# Optimizing a Trainium2 kernel written in Bass

```python
import numpy as np
import jax
import jax.numpy as jnp

def _softmax(x, axis=-1):
    return jax.nn.softmax(x, axis=axis)
def _gelu(x):
    return jax.nn.gelu(x, approximate=True)
def _silu(x):
    return jax.nn.silu(x)
def _sigmoid(x):
    return jax.nn.sigmoid(x)
def _layernorm(x, axis=-1, eps=1e-5):
    m = jnp.mean(x, axis=axis, keepdims=True)
    v = jnp.var(x, axis=axis, keepdims=True)
    return (x - m) / jnp.sqrt(v + eps)
def _scatter_add(tgt, idx, src, axis=0):
    return tgt.at[idx].add(src)
def _segment_sum(src, seg, n):
    return jax.ops.segment_sum(src, seg, n)

kernel_name = 'mk_conv_seq_d2_conv_nhwc64_f43b41'

def setup_inputs(seed: int = 0):
    np.random.seed(seed)
    _w = jnp.asarray
    def _rec_inputs():
        import jax
        import jax.numpy as jnp
        _gk = jax.random.key(seed)
        x = -0.0005207 + 1.001 * jax.random.normal(jax.random.fold_in(_gk, 1), (8, 64, 64, 64), jnp.float32)
        return x
    x = _rec_inputs()
    def _L0_conv_setup():
        import jax, jax.numpy as jnp
        import numpy as np
        B, H, W, C = (8, 64, 64, 64)
        CK = C // 8
        key = jax.random.key(seed)
        ks = jax.random.split(key, 5)
        x = jax.random.normal(ks[0], (B, H, W, C), dtype=jnp.float32)
        wf = jax.random.normal(ks[1], (C, CK), dtype=jnp.float32) * (1.0 / np.sqrt(C))
        bf = jnp.zeros((CK,), dtype=jnp.float32)
        wg = jax.random.normal(ks[2], (C, CK), dtype=jnp.float32) * (1.0 / np.sqrt(C))
        bg = jnp.zeros((CK,), dtype=jnp.float32)
        wh = jax.random.normal(ks[3], (C, C), dtype=jnp.float32) * (1.0 / np.sqrt(C))
        bh = jnp.zeros((C,), dtype=jnp.float32)
        gamma = jax.random.uniform(ks[4], (), dtype=jnp.float32)
        return {'x': x, 'wf': wf, 'bf': bf, 'wg': wg, 'bg': bg, 'wh': wh, 'bh': bh, 'gamma': gamma}
    _L0_conv_all = _L0_conv_setup()
    _L0_conv_in = {k: v for k, v in _L0_conv_all.items() if k in ('wf', 'bf', 'wg', 'bg', 'wh', 'bh', 'gamma', )}
    del _L0_conv_all

    def _L1_conv_setup():
        import jax, jax.numpy as jnp
        import numpy as np
        B, Hh, Ww, C = (4, 64, 64, 64)
        key = jax.random.key(seed)
        ks = jax.random.split(key, 5)
        scale = 1.0 / np.sqrt(C)
        return {'x': jax.random.normal(ks[0], (B, Hh, Ww, C), dtype=jnp.float32), 'Wq': jax.random.normal(ks[1], (C, C), dtype=jnp.float32) * scale, 'bq': jnp.zeros((C,), dtype=jnp.float32), 'Wk': jax.random.normal(ks[2], (C, C), dtype=jnp.float32) * scale, 'bk': jnp.zeros((C,), dtype=jnp.float32), 'Wv': jax.random.normal(ks[3], (C, C), dtype=jnp.float32) * scale, 'bv': jnp.zeros((C,), dtype=jnp.float32), 'gamma': jax.random.normal(ks[4], (1,), dtype=jnp.float32) * 0.05}
    _L1_conv_all = _L1_conv_setup()
    _L1_conv_in = {k: v for k, v in _L1_conv_all.items() if k in ('Wq', 'bq', 'Wk', 'bk', 'Wv', 'bv', 'gamma', )}
    del _L1_conv_all

    return {
        "x": x,
        "L0_conv_wf": _L0_conv_in["wf"],
        "L0_conv_bf": _L0_conv_in["bf"],
        "L0_conv_wg": _L0_conv_in["wg"],
        "L0_conv_bg": _L0_conv_in["bg"],
        "L0_conv_wh": _L0_conv_in["wh"],
        "L0_conv_bh": _L0_conv_in["bh"],
        "L0_conv_gamma": _L0_conv_in["gamma"],
        "L1_conv_Wq": _L1_conv_in["Wq"],
        "L1_conv_bq": _L1_conv_in["bq"],
        "L1_conv_Wk": _L1_conv_in["Wk"],
        "L1_conv_bk": _L1_conv_in["bk"],
        "L1_conv_Wv": _L1_conv_in["Wv"],
        "L1_conv_bv": _L1_conv_in["bv"],
        "L1_conv_gamma": _L1_conv_in["gamma"],
    }

def reference(x, L0_conv_wf, L0_conv_bf, L0_conv_wg, L0_conv_bg, L0_conv_wh, L0_conv_bh, L0_conv_gamma, L1_conv_Wq, L1_conv_bq, L1_conv_Wk, L1_conv_bk, L1_conv_Wv, L1_conv_bv, L1_conv_gamma):
    import jax
    import jax.numpy as jnp
    def _L0_conv_ref(x, wf, bf, wg, bg, wh, bh, gamma):
        import jax, jax.numpy as jnp
        import numpy as np
        B, H, W, C = (8, 64, 64, 64)
        CK = C // 8
        b, h, w, c = x.shape
        n = h * w
        xf = x.reshape(b, n, c)
        f = xf @ wf + bf
        g = xf @ wg + bg
        hh = xf @ wh + bh
        s = jnp.einsum('bnk,bmk->bnm', g, f)
        attn = jax.nn.softmax(s, axis=-1)
        o = jnp.einsum('bnm,bmc->bnc', attn, hh)
        return gamma * o.reshape(b, h, w, c) + x

    def _L1_conv_ref(x, Wq, bq, Wk, bk, Wv, bv, gamma):
        import jax, jax.numpy as jnp
        import numpy as np
        B, Hh, Ww, C = (4, 64, 64, 64)
        b, h, w, c = x.shape
        n = h * w
        q = (jnp.einsum('bhwc,cf->bhwf', x, Wq) + bq).reshape(b, n, c)
        k = (jnp.einsum('bhwc,cf->bhwf', x, Wk) + bk).reshape(b, n, c)
        v = (jnp.einsum('bhwc,cf->bhwf', x, Wv) + bv).reshape(b, n, c)
        energy = jnp.einsum('bic,bjc->bij', q, k)
        attn = jax.nn.softmax(energy, axis=-1)
        out = jnp.einsum('bmn,bmc->bnc', attn, v)
        out = out.reshape(b, h, w, c)
        return gamma * out + x

    def _gn(v, G=32, eps=1e-5):
        B_, H_, W_, C_ = v.shape
        g = v.reshape(B_, H_, W_, G, C_ // G)
        m = jnp.mean(g, axis=(1, 2, 4), keepdims=True)
        s = jnp.var(g, axis=(1, 2, 4), keepdims=True)
        return ((g - m) / jnp.sqrt(s + eps)).reshape(v.shape)

    def _ln_c(v, eps=1e-6):
        m = jnp.mean(v, axis=-1, keepdims=True)
        s = jnp.var(v, axis=-1, keepdims=True)
        return (v - m) / jnp.sqrt(s + eps)

    def _ln_t(v, eps=1e-5):
        m = jnp.mean(v, axis=-1, keepdims=True)
        s = jnp.var(v, axis=-1, keepdims=True)
        return (v - m) / jnp.sqrt(s + eps)

    def _to_tokens(v):
        B_, H_, W_, C_ = v.shape
        return v.reshape(B_, H_ * W_, C_)
    def _from_tokens(t, like):
        return t.reshape(like.shape)

    x = _L0_conv_ref(x, L0_conv_wf, L0_conv_bf, L0_conv_wg, L0_conv_bg, L0_conv_wh, L0_conv_bh, L0_conv_gamma)
    x = _L1_conv_ref(x, L1_conv_Wq, L1_conv_bq, L1_conv_Wk, L1_conv_bk, L1_conv_Wv, L1_conv_bv, L1_conv_gamma)
    return x


_drawn_inputs = setup_inputs


def setup_inputs(seed=0):
    import zlib

    import numpy as np

    out = dict(_drawn_inputs(seed))
    spreads = {'L0_conv_bf': (0.0, 0.8),
     'L0_conv_bg': (0.0, 0.722),
     'L0_conv_bh': (0.0, 0.522),
     'L1_conv_bq': (0.0, 0.662),
     'L1_conv_bk': (0.0, 0.8),
     'L1_conv_bv': (0.0, 0.544)}
    factors = {}
    for name, (base, spread) in spreads.items():
        noise = np.random.default_rng([zlib.crc32(name.encode()), seed]).standard_normal(out[name].shape)
        drawn = base * np.exp(spread * noise) if base else spread * noise
        out[name] = jnp.asarray(drawn.astype(out[name].dtype))
    for name, factor in factors.items():
        out[name] = (out[name] * factor).astype(out[name].dtype)
    return out
```

```python
import math
from contextlib import ExitStack

import concourse.bass as bass
from concourse import mybir

F32 = mybir.dt.float32
F16 = mybir.dt.float16
BF16 = mybir.dt.bfloat16
I32 = mybir.dt.int32
ALU = mybir.AluOpType
ACT = mybir.ActivationFunctionType
AX_X = mybir.AxisListType.X
ds = bass.ds

P = 128
BANK = 512
EXPONENT_BITS = 0x7F800000
EXP_UP = 15
LOG_UP = EXP_UP * math.log(2.0)
HALF_TOP = 14


def attention_pair_kernel(nc, x, wf, bf, wg, bg, wh, bh, gamma0, wq, bq, wk, bk, wv, bv, gamma1, out):
    B, H, W, C = x.shape
    N = H * W
    CK = wf.shape[1]
    T = N // P
    C1 = C + 1
    NQ = N // BANK
    CH = 2 * BANK
    NCH = N // CH
    BPC = CH // P
    KS = 9 * CK
    KM = KS + 3
    MROW = 64
    GFW = 2 * CK
    PW = GFW + C
    VW = C + 1
    TR = BANK // P
    RND = T // TR
    RT = T // BPC
    ATN = N // BANK
    ATS = T * ATN
    U0 = 8
    U1 = 2 * NCH
    RING = 4
    LAG0 = 5
    LAG1 = 7
    STEPS0, STEPS1 = NCH * T, T * NCH
    HIGH = [{"act": [0, 1, 2], "pool": [3]}, {"act": [0, 1], "pool": [2]}]
    LOW = [{"dve": [0, 1], "pool": [2, 3]}, {"pool": [0, 1, 2]}]
    WHOLE = 3
    DVE_BEHIND = 2
    FREE_ST, FREE_A, FREE_E0, FREE_S1, FREE_E1 = 2, 2, U0, 2, U1
    FREE_LOW = RING
    FREE = 1
    assert N % (P * BPC) == 0 and C == 64 and CK == 8 and NCH == 4

    x_t = x.rearrange("b h w c -> b (h w) c").rearrange("b (p t) c -> b p t c", p=P)
    out_t = out.rearrange("b h w c -> b (h w) c").rearrange("b (p t) c -> b p t c", p=P)

    with ExitStack() as ctx:
        def sb(name, shape, dt):
            return ctx.enter_context(nc.sbuf_tensor(name, shape, dt))

        def sem(name):
            return ctx.enter_context(nc.semaphore(name))

        score_banks = ctx.enter_context(nc.psum_tensor("score_banks", [P, 4, BANK], F32))
        sum_banks = ctx.enter_context(nc.psum_tensor("sum_banks", [P, 4, BANK], F32))

        x_in = sb("x_in", [P, T, C], F32)
        x_mid = sb("x_mid", [P, T, C], F32)
        y = sb("y", [P, T, C], F32)
        x_tr = sb("x_tr", [C1, N], F32)
        w0 = sb("w0", [C1, PW], F32)
        w1 = sb("w1", [C1, 4, C], F32)
        w1s = sb("w1s", [C1, 4 * C], F32)
        w1v = sb("w1v", [C1, C], F32)
        w_row = sb("w_row", [C1, 1], F32)
        x_abs = sb("x_abs", [C1, 1], F32)
        bound_in = sb("bound_in", [C1, 1], F32)
        gammas = sb("gammas", [P, 2], F32)
        ident = sb("ident", [P, P], F32)
        ident_b = sb("ident_b", [P, P], BF16)
        ones = sb("ones", [C1, 1], F32)
        zeros = sb("zeros", [P, BANK], F16)
        ones_b = sb("ones_b", [P, 1], BF16)
        credit = sb("credit", [P, 12], F32)
        proj = sb("proj", [P, T, PW + 1], F32)
        piece = [sb(f"piece{k}", [P, T, GFW], BF16) for k in range(3)]
        rest = [sb(f"rest{k}", [P, T, GFW], F32) for k in range(2)]
        g_stack = sb("g_stack", [P, T, P], BF16)
        f_stack = sb("f_stack", [P, T, P], BF16)
        g_tr = sb("g_tr", [KM, N], BF16)
        f_tr = sb("f_tr", [KM, N], BF16)
        tile_max = sb("tile_max", [P, BPC, ATN], F32)
        row_max0 = sb("row_max0", [P, BPC], F32)
        max_rest = sb("max_rest", [P, BPC], F32)
        inv_sum0 = sb("inv_sum0", [P, 2, BPC // 2], F32)
        inv_gam0 = sb("inv_gam0", [P, 2, BPC // 2], F32)
        att0 = sb("att0", [P, BPC, C], F32)
        probs = sb("probs", [P, RING, CH], F32)
        e_high = sb("e_high", [P, U1, CH], F16)
        e_whole = sb("e_whole", [P, U1 // 4, CH], F32)
        e_low = sb("e_low", [P, U1, CH], F16)
        h_scaled = sb("h_scaled", [P, T, C], F32)
        h_high = sb("h_high", [P, T, VW], F16)
        h_low = sb("h_low", [P, T, C], F16)
        v_abs = sb("v_abs", [P, 2], F32)
        v_top = sb("v_top", [P, 2], F32)
        v_top1 = sb("v_top1", [P, 2], F32)
        v_pow2 = sb("v_pow2", [P, 2], F32)
        v_inv = sb("v_inv", [P, 2], F32)
        v_up = sb("v_up", [P, 2], F32)
        gam_down = sb("gam_down", [P, 2], F32)
        q_split = sb("q_split", [P, N], F16)
        k_high = sb("k_high", [P, N], F16)
        k_low = sb("k_low", [P, N], F16)
        v1 = sb("v1", [P, T, C], F32)
        v_scaled = sb("v_scaled", [P, 2, NCH, C], F32)
        v_high = sb("v_high", [P, 2, NCH, C], F16)
        v_low = sb("v_low", [P, 2, NCH, C], F16)
        log_up = sb("log_up", [P, 1], F32)
        bound = sb("bound", [P, 1], F32)
        pow2 = sb("pow2", [P, 1], F32)
        inv_pow2 = sb("inv_pow2", [P, 1], F32)
        up = sb("up", [P, 1], F32)
        down1 = sb("down1", [P, 1], F32)
        down = sb("down", [P, 1], F32)
        neg_down = sb("neg_down", [P, 1], F32)
        chunk_max = sb("chunk_max", [P, 2, NCH], F32)
        exp_bias = sb("exp_bias", [P, U1], F32)
        row_max1 = sb("row_max1", [P, 2], F32)
        below_max = sb("below_max", [P, 2, NCH], F32)
        chunk_w = sb("chunk_w", [P, 2, NCH], F32)
        part_sum = sb("part_sum", [P, 2, NCH], F32)
        part_scr = sb("part_scr", [P, NCH], F32)
        row_sum1 = sb("row_sum1", [P, 2], F32)
        inv_sum1 = sb("inv_sum1", [P, 2], F32)
        norm_w = sb("norm_w", [P, 2, NCH], F32)

        w_in, x_loaded, y_stored = sem("w_in"), sem("x_loaded"), sem("y_stored")
        ident_zero, ident_f, ident_ready, const_ready = sem("ident_zero"), sem("ident_f"), sem("ident_ready"), sem("const_ready")
        w_ready = sem("w_ready")
        xt_ps, xt_act, xt_dve = sem("xt_ps"), sem("xt_act"), sem("xt_dve")
        pj_ps, pj_act, pj_dve = sem("pj_ps"), sem("pj_act"), sem("pj_dve")
        piece_ready, g_stacked, f_stacked = sem("piece_ready"), sem("g_stacked"), sem("f_stacked")
        ft_ps, gt_ps, ft_sb, gt_sb = sem("ft_ps"), sem("gt_ps"), sem("ft_sb"), sem("gt_sb")
        a_ready, a_used = sem("a_ready"), sem("a_used")
        max_split, mrow_ps, mrow_sb = sem("max_split"), sem("mrow_ps"), sem("mrow_sb")
        st_ready, exp0_done, pv0_done = sem("st_ready"), sem("exp0_done"), sem("pv0_done")
        att0_ready, x_mid_ready = sem("att0_ready"), sem("x_mid_ready")
        bound_sent, bound_ps, w1s_ready = sem("bound_sent"), sem("bound_ps"), sem("w1s_ready")
        v1_ps, v1_sb = sem("v1_ps"), sem("v1_sb")
        qk_ps, high_done, low_done = sem("qk_ps"), sem("high_done"), sem("low_done")
        s_ready, bias_ready, exp1_done, pv1_done = sem("s_ready"), sem("bias_ready"), sem("exp1_done"), sem("pv1_done")
        below_ready, chunk_w_ready, y_ready = sem("below_ready"), sem("chunk_w_ready"), sem("y_ready")
        dve_step = sem("dve_step")
        high_by = {"act": sem("high_by_act"), "pool": sem("high_by_pool")}
        low_by = {"dve": sem("low_by_dve"), "pool": sem("low_by_pool")}
        v_abs_ready, v_top_ready, h_scale_ready = sem("v_abs_ready"), sem("v_top_ready"), sem("h_scale_ready")
        h_scaled_ready, h_high_ready, h_low_ready = sem("h_scaled_ready"), sem("h_high_ready"), sem("h_low_ready")
        v_split_ready = sem("v_split_ready")
        pool_go = sem("pool_go")

        block = ctx.enter_context(nc.Block())
        N_W = 18

        def wait_x_tr(eng, image, layer):
            eng.wait_ge(xt_act, (image * 2 + layer + 1) * RT)
            eng.wait_ge(xt_dve, (image * 2 + layer + 1) * RT)

        def half_of_blocks(r, odd):
            return x_tr[0:C, r * CH:(r + 1) * CH].rearrange("c (k a n) -> c k a n", a=2, n=P)[:, :, odd, :]

        def part_done(table, sems, layer, image, k4, u, wraps_back=0):
            by = next(e for e, slots in table[layer].items() if u % 4 in slots)
            n = [len(table[l].get(by, [])) for l in range(2)]
            before = n[0] * STEPS0 // 4 if layer == 1 else 0
            rank = table[layer][by].index(u % 4) + 1
            return sems[by], image * ((n[0] * STEPS0 + n[1] * STEPS1) // 4) + before + (k4 - wraps_back) * n[layer] + rank

        def wait_high(eng, layer, image, k4, u):
            eng.wait_ge(*part_done(HIGH, high_by, layer, image, k4, u))

        def wait_low(eng, layer, image, k4, u, ago=0):
            done, count = part_done(LOW, low_by, layer, image, k4, u, ago)
            eng.wait_ge(done, count + FREE_LOW)

        def split_high(copy, slot, u):
            return copy(e_high[:, slot, :], probs[:, u % RING, :])

        def split_low(subtract, slot, u):
            return subtract(e_low[:, slot, :], probs[:, u % RING, :], e_high[:, slot, :], ALU.subtract)

        @block.sync
        def _(sp):
            for col, w_, b_ in ((0, wg, bg), (CK, wf, bf), (GFW, wh, bh)):
                n = w_.shape[1]
                sp.dma_start(w0[0:C, col:col + n], w_).then_inc(w_in, 16)
                sp.dma_start(w0[C:C1, col:col + n], b_.unsqueeze(0)).then_inc(w_in, 16)
            sp.dma_start(x_in[:, :, :], x_t[0]).then_inc(x_loaded, 16)
            for k, w_, b_ in ((0, wq, bq), (1, wq, bq), (2, wk, bk), (3, wk, bk)):
                sp.dma_start(w1[0:C, k, :], w_).then_inc(w_in, 16)
                if k % 2 == 0:
                    continue
                sp.dma_start(w1[C:C1, k - 1, :], b_.unsqueeze(0)).then_inc(w_in, 16)
                sp.dma_start(w1[C:C1, k, :], b_.unsqueeze(0)).then_inc(w_in, 16)
            sp.dma_start(w1v[0:C, :], wv).then_inc(w_in, 16)
            sp.dma_start(w1v[C:C1, :], bv.unsqueeze(0)).then_inc(w_in, 16)
            sp.dma_start(gammas[:, 0:1], gamma0.partition_broadcast(P)).then_inc(w_in, 16)
            sp.dma_start(gammas[:, 1:2], gamma1.partition_broadcast(P)).then_inc(w_in, 16)

            def store(image):
                for j in range(NCH):
                    sp.wait_ge(y_ready, image * NCH + j + 1 + FREE)
                    sp.dma_start(out_t[image, :, j * BPC:(j + 1) * BPC, :],
                                 y[:, j * BPC:(j + 1) * BPC, :]).then_inc(y_stored, 16)

            with sp.Fori(0, B - 1) as image:
                sp.wait_ge(x_mid_ready, (image + 1) * NCH + FREE)
                sp.dma_start(x_in[:, :, :], x_t[image + 1]).then_inc(x_loaded, 16)
                store(image)
            store(B - 1)
            sp.wait_ge(y_stored, 16 * (NCH * B + FREE))

        @block.gpsimd
        def _(pool):
            nc.gpsimd.memset(ident[:], 0.0).then_inc(ident_zero, 1)
            pool.wait_ge(ident_zero, 1)
            nc.gpsimd.affine_select(out=ident[:], in_=ident[:], compare_op=ALU.not_equal, fill=1.0, base=0,
                                    pattern=[[-1, P]], channel_multiplier=1).then_inc(ident_f, 1)
            pool.wait_ge(ident_f, 1)
            nc.gpsimd.tensor_copy(ident_b[:], ident[:]).then_inc(ident_ready, 1)
            nc.gpsimd.memset(g_stack[:], 0.0).then_inc(const_ready, 1)
            nc.gpsimd.memset(f_stack[:], 1.0).then_inc(const_ready, 1)
            nc.gpsimd.memset(proj[:, :, PW:PW + 1], 1.0).then_inc(const_ready, 1)
            nc.gpsimd.memset(ones[:], 1.0).then_inc(const_ready, 1)
            nc.gpsimd.memset(ones_b[:], 1.0).then_inc(const_ready, 1)
            nc.gpsimd.memset(credit[:, 0:1], 0.0).then_inc(exp0_done, FREE_ST)
            nc.gpsimd.memset(credit[:, 1:2], 0.0).then_inc(a_used, FREE_A)
            nc.gpsimd.memset(credit[:, 2:3], 0.0).then_inc(pv0_done, FREE_E0)
            nc.gpsimd.memset(credit[:, 3:4], 0.0).then_inc(exp1_done, FREE_S1)
            nc.gpsimd.memset(credit[:, 4:5], 0.0).then_inc(pv1_done, FREE_E1)
            nc.gpsimd.memset(credit[:, 5:6], 0.0).then_inc(low_by["pool"], FREE_LOW)
            nc.gpsimd.memset(credit[:, 6:7], 0.0).then_inc(low_by["dve"], FREE_LOW)
            nc.gpsimd.memset(log_up[:], LOG_UP).then_inc(const_ready, 1)
            for n, (free, by) in enumerate(((y_ready, FREE), (att0_ready, FREE), (x_mid_ready, FREE), (y_stored, 16 * FREE))):
                nc.gpsimd.memset(credit[:, 8 + n:9 + n], 0.0).then_inc(free, by)
            nc.gpsimd.memset(zeros[:], 0.0).then_inc(const_ready, 1)
            nc.gpsimd.memset(h_high[:, :, C:VW], 1.0).then_inc(const_ready, 1)
            pool.wait_ge(const_ready, 10)

            def largest_value(image, layer):
                pool.wait_ge(v_abs_ready, image * 2 + layer + 1)
                pool.sem_inc(pool_go, 1)
                nc.gpsimd.partition_all_reduce(v_top[:, layer:layer + 1], v_abs[:, layer:layer + 1], P,
                                               bass.bass_isa.ReduceOp.max).then_inc(v_top_ready, 1)

            def split(layer, image, k, k4, u, slot):
                high, low = u % 4 in HIGH[layer]["pool"], u % 4 in LOW[layer]["pool"]
                step = image * STEPS0 + k
                if high:
                    pool.wait_ge(*((exp0_done, step + 1 + FREE_ST) if layer == 0 else (exp1_done, step + 1 + FREE_S1)))
                    pool.wait_ge(pv0_done if layer == 0 else pv1_done, step + 1)
                    pool.sem_inc(pool_go, 1)
                    split_high(lambda o, i: nc.gpsimd.tensor_scalar(o, i, 1.0, 0.0, ALU.mult, ALU.add), slot, u
                               ).then_inc(high_by["pool"], 1)
                if low:
                    wait_high(pool, layer, image, k4, u)
                    split_low(nc.gpsimd.tensor_tensor, slot, u).then_inc(low_by["pool"], 1)

            def steps1(image, t):
                for u in range(U1):
                    split(1, image, t * U1 + u, t * 2 + u // 4, u, u)

            with pool.Fori(0, B) as image:
                for k in range(3):
                    pool.wait_ge(piece_ready, image * 3 + k + 1)
                    dst = g_stack[:, :, 3 * CK * k:3 * CK * (k + 1)].rearrange("p t (r c) -> p t r c", r=3)
                    src = piece[k][:, :, 0:CK].unsqueeze(2).to_broadcast([P, T, 3, CK])
                    one = ones_b[:, :].unsqueeze(2).unsqueeze(3).to_broadcast([P, T, 3, CK])
                    nc.gpsimd.tensor_tensor(dst, src, one, ALU.mult).then_inc(g_stacked, 1)
                largest_value(image, 0)
                for r in range(NCH):
                    blocks = slice(r * BPC, (r + 1) * BPC)
                    pool.wait_ge(h_high_ready, image * NCH + r + 1)
                    nc.gpsimd.tensor_tensor(h_low[:, blocks, :], h_scaled[:, blocks, :], h_high[:, blocks, 0:C],
                                            ALU.subtract).then_inc(h_low_ready, 1)
                with pool.Fori(0, NCH) as q:
                    with pool.Fori(0, T // U0) as t:
                        for u in range(U0):
                            split(0, image, q * T + t * U0 + u, q * (T // 4) + t * (U0 // 4) + u // 4, u, u)
                    pool.wait_ge(att0_ready, image * NCH + q + 1 + FREE)
                    nc.gpsimd.tensor_tensor(x_mid[:, ds(q * BPC, BPC), :], att0[:, :, :],
                                            x_in[:, ds(q * BPC, BPC), :], ALU.add).then_inc(x_mid_ready, 1)
                largest_value(image, 1)
                with pool.Fori(0, T // 2) as t:
                    steps1(image, t)

        @block.tensor
        def _(pe):
            def transposes(image, layer, src):
                for r in range(RT):
                    if layer == 1:
                        pe.wait_ge(x_mid_ready, image * NCH + r + 1 + FREE)
                    for k in range(BPC // 2):
                        t = r * BPC + 2 * k
                        mm = nc.tensor.transpose(score_banks[:, r, k * P:(k + 1) * P],
                                                 src[:, t:t + 2, :].rearrange("p a c -> p (a c)"), ident[:, :])
                    mm.then_inc(xt_ps, 1)

            def max_pass_tile(image, blk, j):
                tile = image * ATS + blk * ATN + j
                pe.wait_ge(a_used, tile + 1)
                nc.tensor.matmul(sum_banks[:, 2 + j % 2, :], g_tr[0:KS, ds(blk * P, P)],
                                 f_tr[0:KS, j * BANK:(j + 1) * BANK], start=True, stop=True).then_inc(a_ready, 1)

            def max_rows(image, q):
                pe.wait_ge(max_split, image * NCH + q + 1)
                for k in range(BPC):
                    mm = nc.tensor.matmul(sum_banks[:, 2 + k // 4, (k % 4) * P:(k % 4 + 1) * P],
                                          g_stack[:, q * BPC + k, :], ident_b[:, :], start=True, stop=True)
                mm.then_inc(mrow_ps, 1)

            def scores0(image, q, i, u):
                step = image * NCH * T + q * T + i
                pe.wait_ge(exp0_done, step + 1)
                for h in range(2):
                    mm = nc.tensor.matmul(score_banks[:, 2 * (u % 2) + h, :], f_tr[0:KM, ds(i * P, P)],
                                          g_tr[0:KM, ds(q * CH + h * BANK, BANK)], start=True, stop=True)
                mm.then_inc(st_ready, 1)

            def products(low_slot, bank_of, width, pitch, highs, lows):
                for n in range(BPC):
                    bank, o = bank_of(n)
                    for e in (e_high, e_low):
                        for v in (highs, lows):
                            mm = nc.tensor.matmul(sum_banks[:, bank, o:o + v.shape[-1]], e[:, low_slot, n * P:(n + 1) * P],
                                                  v, start=False, stop=True, skip_group_check=True)
                return mm

            def open_sums(banks):
                for j in range(banks):
                    nc.tensor.matmul(sum_banks[:, j, :], zeros[:, 0:P], zeros[:, :], start=True, stop=True,
                                     skip_group_check=True)

            def values0(image, q, i, k4, u):
                wait_low(pe, 0, image, k4, u)
                products(u % U0, lambda n: (n // 4, (n % 4) * VW), VW, VW,
                         h_high[:, i, :], h_low[:, i, :]).then_inc(pv0_done, 1)

            def chunk0(image, q, next_max):
                pe.wait_ge(mrow_sb, image * NCH + q + 1)
                pe.wait_ge(att0_ready, image * NCH + q + FREE)

                pe.wait_ge(h_low_ready, (image + 1) * NCH)
                open_sums(2)

                def steps(t, first):
                    for u in range(U0):
                        i = t * U0 + u
                        scores0(image, q, i, u)
                        if next_max:
                            for j in range(2 * (u % 4), 2 * (u % 4) + 2):
                                max_pass_tile(image, (q + 1) * BPC + t * (U0 // 4) + u // 4, j)
                        if not first or u >= LAG0:
                            values0(image, q, i - LAG0, q * (T // 4) + t * (U0 // 4) + (u - LAG0) // 4, u - LAG0)

                steps(0, True)
                with pe.Fori(1, T // U0) as t:
                    steps(t, False)
                for i in range(T - LAG0, T):
                    values0(image, q, i, q * (T // 4) + i // 4, i)
                if next_max:
                    max_rows(image, q + 1)

            def scores1(image, i, k, u):
                pe.wait_ge(exp1_done, image * STEPS1 + k + 1)
                for h in range(2):
                    col = (u % NCH) * CH + h * BANK
                    bank = score_banks[:, 2 * (u % 2) + h, :]
                    nc.tensor.matmul(bank, q_split[:, ds(i * P, P)], k_high[:, col:col + BANK], start=True, stop=False)
                    mm = nc.tensor.matmul(bank, q_split[:, ds(i * P, P)], k_low[:, col:col + BANK],
                                          start=False, stop=True)
                mm.then_inc(s_ready, 1)

            def values1(image, i, k4, u):
                u, j = u % U1, u % NCH
                if j == 0:
                    pe.wait_ge(v_split_ready, image * T + i + 1)
                if j == WHOLE:
                    pe.wait_ge(exp1_done, image * STEPS1 + k4 * 4 + j + 1 + FREE_S1)
                    for n in range(BPC):
                        mm = nc.tensor.matmul(sum_banks[:, j, n * C:(n + 1) * C], e_whole[:, u // 4, n * P:(n + 1) * P],
                                              v_scaled[:, u // NCH, j, :], start=False, stop=True,
                                              skip_group_check=True)
                    mm.then_inc(pv1_done, 1)
                    return
                wait_low(pe, 1, image, k4, u)
                products(u, lambda n: (j, n * C), C, C, v_high[:, u // NCH, j, :],
                         v_low[:, u // NCH, j, :]).then_inc(pv1_done, 1)

            pe.wait_ge(ident_ready, 1)
            pe.wait_ge(const_ready, 10)
            pe.wait_ge(w_in, 16 * N_W)
            with pe.Fori(0, B) as image:
                pe.wait_ge(x_loaded, 16 * (image + 1))
                pe.wait_ge(exp1_done, image * STEPS1 + FREE_S1)
                transposes(image, 0, x_in)
                wait_x_tr(pe, image, 0)
                for r in range(RND):
                    if r >= 4:
                        pe.wait_ge(pj_act if r % 2 == 0 else pj_dve, image * (RND // 2) + (r - 4) // 2 + 1)
                    for k in range(TR):
                        t = r * TR + k
                        mm = nc.tensor.matmul(score_banks[:, r % 4, k * P:k * P + PW], x_tr[:, t * P:(t + 1) * P],
                                              w0[:, :], start=True, stop=True)
                    mm.then_inc(pj_ps, 1)
                pe.wait_ge(pj_act, (image + 1) * (RND // 2))
                pe.wait_ge(pj_dve, (image + 1) * (RND // 2))
                pe.wait_ge(y_ready, image * NCH + FREE)
                for r in range(NCH):
                    for src, stacked, used, ready, which in ((f_stack, f_stacked, ft_sb, ft_ps, 0),
                                                             (g_stack, g_stacked, gt_sb, gt_ps, 1)):
                        if r == 0:
                            pe.wait_ge(stacked, (image + 1) * 3)
                        if r >= 2:
                            pe.wait_ge(used, image * NCH + r - 1)
                        bank = score_banks[0:KM, 2 * (r % 2) + which, :].bitcast(BF16)
                        rows = KM if which == 0 else KS
                        for k in range(BPC):
                            mm = nc.tensor.transpose(bank[0:rows, k * P:(k + 1) * P],
                                                     src[:, r * BPC + k, 0:rows], ident_b[:, :])
                        mm.then_inc(ready, 1)
                with pe.Fori(0, BPC) as blk:
                    pe.wait_ge(ft_sb, (image + 1) * NCH)
                    pe.wait_ge(gt_sb, (image + 1) * NCH)
                    for j in range(ATN):
                        max_pass_tile(image, blk, j)
                max_rows(image, 0)
                with pe.Fori(0, NCH - 1) as q:
                    chunk0(image, q, True)
                chunk0(image, NCH - 1, False)
                pe.wait_ge(exp0_done, (image + 1) * NCH * T + FREE_ST)
                transposes(image, 1, x_mid)
                wait_x_tr(pe, image, 1)
                for r in range(NCH):
                    for k in range(BPC):
                        t = r * BPC + k
                        mm = nc.tensor.matmul(score_banks[:, r, k * C:(k + 1) * C], x_tr[:, t * P:(t + 1) * P],
                                              w1v[:, :], start=True, stop=True)
                    mm.then_inc(v1_ps, 1)
                pe.wait_ge(bound_sent, image + 1)
                nc.tensor.matmul(sum_banks[:, 0, 0:1], bound_in[:, :].to_broadcast([C1, P]), ones[:, :],
                                 start=True, stop=True).then_inc(bound_ps, 1)
                pe.wait_ge(w1s_ready, image + 1)
                for c in range(2 * NQ):
                    if c < 4:
                        pe.wait_ge(v1_sb, image * NCH + c + 1)
                    else:
                        pe.wait_ge(low_done, image * 2 * NQ + c - 3)
                    side = 1 - c % 2
                    nc.tensor.matmul(score_banks[:, c % 4, :], w1s[:, side * 2 * C:(side + 1) * 2 * C],
                                     x_tr[:, (c // 2) * BANK:(c // 2 + 1) * BANK],
                                     start=True, stop=True).then_inc(qk_ps, 1)
                pe.wait_ge(low_done, (image + 1) * 2 * NQ)

                open_sums(NCH)

                def steps1(t, first):
                    for u in range(U1):
                        scores1(image, t * 2 + u // NCH, t * U1 + u, u)
                        if not first or u >= LAG1:
                            v = u - LAG1
                            values1(image, t * 2 + v // NCH, t * 2 + v // NCH, v)

                steps1(0, True)
                with pe.Fori(1, T // 2) as t:
                    steps1(t, False)
                for k in range(T * NCH - LAG1, T * NCH):
                    values1(image, k // NCH, k // NCH, k)

        @block.scalar
        def _(act):
            def transposed(image, layer):
                for r in range(RT):
                    act.wait_ge(xt_ps, (image * 2 + layer) * RT + r + 1)
                    nc.scalar.copy(half_of_blocks(r, 0), score_banks[0:C, r, :].rearrange("c (k n) -> c k n", n=P)
                                   ).then_inc(xt_act, 1)

            def max_rows(image, q):
                act.wait_ge(mrow_ps, image * NCH + q + 1)
                nc.scalar.copy(g_tr[MROW:KM, ds(q * CH, CH)].rearrange("p (a n) -> p a n", a=2),
                               sum_banks[MROW:KM, 2:4, :]).then_inc(mrow_sb, 1)

            def chunk0(image, q, next_max):
                with act.Fori(0, T // U0) as t:
                    for u in range(U0):
                        step = image * NCH * T + q * T + t * U0 + u
                        k4 = q * (T // 4) + t * (U0 // 4) + u // 4
                        act.wait_ge(st_ready, step + 1)
                        wait_low(act, 0, image, k4, u, ago=1)
                        nc.scalar.activation(probs[:, u % RING, :].rearrange("p (a n) -> p a n", a=2),
                                             score_banks[:, 2 * (u % 2):2 * (u % 2) + 2, :],
                                             ACT.Exp, bias=log_up[:, 0:1]).then_inc(exp0_done, 1)
                        if u % 4 in HIGH[0]["act"]:
                            act.wait_ge(exp0_done, step + 1 + FREE_ST)
                            act.wait_ge(pv0_done, step + 1)
                            split_high(nc.scalar.copy, u, u).then_inc(high_by["act"], 1)
                if next_max:
                    max_rows(image, q + 1)

            act.wait_ge(const_ready, 10)
            with act.Fori(0, B) as image:
                transposed(image, 0)
                for r in range(0, RND, 2):
                    act.wait_ge(pj_ps, image * RND + r + 1)
                    nc.scalar.copy(proj[:, r * TR:(r + 1) * TR, 0:PW],
                                   score_banks[:, r % 4, :].rearrange("p (k n) -> p k n", k=TR)[:, :, 0:PW]
                                   ).then_inc(pj_act, 1)
                for k in range(3):
                    act.wait_ge(piece_ready, image * 3 + k + 1)
                    dst = f_stack[:, :, 0:KS].rearrange("p t (r k c) -> p t r k c", r=3, k=3)[:, :, :, k, :]
                    src = piece[k][:, :, CK:GFW].unsqueeze(2).to_broadcast([P, T, 3, CK])
                    nc.scalar.copy(dst, src).then_inc(f_stacked, 1)
                for r in range(NCH):
                    act.wait_ge(ft_ps, image * NCH + r + 1)
                    nc.scalar.copy(f_tr[0:KM, r * CH:(r + 1) * CH],
                                   score_banks[0:KM, 2 * (r % 2), :].bitcast(BF16)).then_inc(ft_sb, 1)
                for r in range(NCH):
                    blocks = slice(r * BPC, (r + 1) * BPC)
                    act.wait_ge(h_scale_ready, image + 1)
                    nc.scalar.activation(h_scaled[:, blocks, :], proj[:, blocks, GFW:PW], ACT.Copy,
                                         scale=v_up[:, 0:1]).then_inc(h_scaled_ready, 1)
                for r in range(NCH):
                    blocks = slice(r * BPC, (r + 1) * BPC)
                    act.wait_ge(h_scaled_ready, image * NCH + r + 1)
                    nc.scalar.copy(h_high[:, blocks, 0:C], h_scaled[:, blocks, :]).then_inc(h_high_ready, 1)
                max_rows(image, 0)
                with act.Fori(0, NCH - 1) as q:
                    chunk0(image, q, True)
                chunk0(image, NCH - 1, False)

                transposed(image, 1)
                for r in range(NCH):
                    act.wait_ge(v1_ps, image * NCH + r + 1)
                    nc.scalar.copy(v1[:, r * BPC:(r + 1) * BPC, :],
                                   score_banks[:, r, :].rearrange("p (k c) -> p k c", k=BPC)).then_inc(v1_sb, 1)
                for c in range(2 * NQ):
                    act.wait_ge(qk_ps, image * 2 * NQ + c + 1)
                    dst = (k_high if c % 2 == 0 else q_split)[:, (c // 2) * BANK:(c // 2 + 1) * BANK]
                    nc.scalar.copy(dst, score_banks[:, c % 4, :]).then_inc(high_done, 1)
                with act.Fori(0, T // 2) as t:
                    for u in range(U1):
                        step = image * STEPS1 + t * U1 + u
                        k4 = t * 2 + u // 4
                        act.wait_ge(bias_ready, step + 1)
                        if u % 4 == WHOLE:
                            act.wait_ge(pv1_done, step + 1)
                            dst = e_whole[:, u // 4, :]
                        else:
                            wait_low(act, 1, image, k4, u, ago=1)
                            dst = probs[:, u % RING, :]
                        nc.scalar.activation(dst.rearrange("p (a n) -> p a n", a=2),
                                             score_banks[:, 2 * (u % 2):2 * (u % 2) + 2, :],
                                             ACT.Exp, bias=exp_bias[:, u:u + 1], scale=down[:, 0:1],
                                             accum_out=part_sum[:, u // NCH, u % NCH:u % NCH + 1]
                                             ).then_inc(exp1_done, 1)
                        if u % 4 in HIGH[1]["act"]:
                            act.wait_ge(exp1_done, step + 1 + FREE_S1)
                            act.wait_ge(pv1_done, step + 1)
                            split_high(nc.scalar.copy, u, u).then_inc(high_by["act"], 1)
                        if u % NCH == NCH - 1:
                            par = u // NCH
                            act.wait_ge(below_ready, image * T + t * 2 + par + 1)
                            nc.scalar.activation(chunk_w[:, par, :], below_max[:, par, :], ACT.Exp
                                                 ).then_inc(chunk_w_ready, 1)

        @block.vector
        def _(dve):
            class Chain:
                base, n = 0, 0

                def link(self, ins):
                    ins.then_inc(dve_step, 1)
                    self.n += 1
                    dve.wait_ge(dve_step, self.base + self.n)

            chain = Chain()

            nc.vector.memset(x_tr[C:C1, :], 1.0).then_inc(const_ready, 1)
            nc.vector.memset(x_abs[C:C1, :], 1.0).then_inc(const_ready, 1)
            dve.wait_ge(w_in, 16 * N_W)
            chain.link(nc.vector.tensor_reduce(w_row[:, :], w1[:, 0:4:2, :], mybir.AxisListType.XY, ALU.add,
                                               apply_absolute_value=True))
            START = chain.n

            LINK_PIECES, LINK_MAX, LINK_ATT = 6, 4, 2
            LINK_BOUND, LINK_CHUNK, LINK_BELOW, LINK_W = 13, 1, 1, 5
            LINK_BLOCK = NCH * LINK_CHUNK + LINK_BELOW + LINK_W
            L0 = LINK_PIECES + NCH * (LINK_MAX + LINK_ATT)
            PER_IMAGE = L0 + LINK_BOUND + T * LINK_BLOCK

            def transposed(image, layer):
                for r in range(RT):
                    dve.wait_ge(xt_ps, (image * 2 + layer) * RT + r + 1)
                    nc.vector.tensor_copy(half_of_blocks(r, 1), score_banks[C:P, r, :]
                                          .rearrange("c (k n) -> c k n", n=P)).then_inc(xt_dve, 1)

            def block_max(image, blk, slot, js):
                for j in js:
                    dve.wait_ge(a_ready, image * ATS + blk * ATN + j + 1)
                    nc.vector.reduce_max(tile_max[:, slot, j:j + 1], sum_banks[:, 2 + j % 2, :], AX_X
                                         ).then_inc(a_used, 1)

            def steps0(image, q, next_max):
                with dve.Fori(0, T // U0) as t:
                    for u in range(U0):
                        if next_max:
                            slot = t * (U0 // 4) + u // 4
                            block_max(image, (q + 1) * BPC + slot, slot, range(2 * (u % 4), 2 * (u % 4) + 2))
                        if (u - DVE_BEHIND) % 4 in LOW[0]["dve"]:
                            low0(image, q * (T // 4) + t * (U0 // 4) + (u - DVE_BEHIND) // 4, u - DVE_BEHIND)

            def low0(image, k4, u):
                wait_high(dve, 0, image, k4, u)
                split_low(nc.vector.tensor_tensor, u, u).then_inc(low_by["dve"], 1)

            def image_scale(image, layer, extra):
                col = slice(layer, layer + 1)
                dve.wait_ge(v_top_ready, image * 2 + layer + 1)
                chain.link(nc.vector.tensor_scalar(v_top1[:, col], v_top[:, col], 2.0 ** -100, None, ALU.max))
                chain.link(nc.vector.tensor_scalar(v_pow2[:, col].bitcast(I32), v_top1[:, col].bitcast(I32),
                                                   EXPONENT_BITS, None, ALU.bitwise_and))
                chain.link(nc.vector.reciprocal(v_inv[:, col], v_pow2[:, col]))
                chain.link(nc.vector.tensor_scalar(gam_down[:, col], v_pow2[:, col], gammas[:, col],
                                                   2.0 ** (extra - HALF_TOP), ALU.mult, ALU.mult))
                up_ = nc.vector.tensor_scalar(v_up[:, col], v_inv[:, col], 2.0 ** (HALF_TOP - extra), None, ALU.mult)
                if layer == 0:
                    up_.then_inc(h_scale_ready, 1)
                else:
                    chain.link(up_)

            def split_max(image, q):
                dve.wait_ge(a_used, image * ATS + (q + 1) * BPC * ATN + FREE_A)
                blocks = ds(q * BPC, BPC)
                chain.link(nc.vector.reduce_max(row_max0[:, :], tile_max[:, :, :], AX_X))
                chain.link(nc.vector.tensor_scalar(g_stack[:, blocks, KS], row_max0[:, :], -1.0, None, ALU.mult))
                chain.link(nc.vector.scalar_tensor_tensor(max_rest[:, :], row_max0[:, :], -1.0,
                                                          g_stack[:, blocks, KS], ALU.mult, ALU.subtract))
                chain.link(nc.vector.tensor_copy(g_stack[:, blocks, KS + 1], max_rest[:, :]))
                nc.vector.tensor_tensor(g_stack[:, blocks, KS + 2], max_rest[:, :], g_stack[:, blocks, KS + 1],
                                        ALU.subtract).then_inc(max_split, 1)

            def attention0(image, q):
                dve.wait_ge(pv0_done, image * NCH * T + (q + 1) * T + FREE_E0)
                dve.wait_ge(x_mid_ready, image * NCH + q + FREE)
                sums = sum_banks[:, 0:2, 0:4 * VW].rearrange("p a (k c) -> p a k c", c=VW)
                chain.link(nc.vector.reciprocal(inv_sum0[:, :, :], sums[:, :, :, C]))
                chain.link(nc.vector.tensor_scalar(inv_gam0[:, :, :], inv_sum0[:, :, :], gam_down[:, 0:1], None, ALU.mult))
                nc.vector.tensor_tensor(att0[:, :, :].rearrange("p (a k) c -> p a k c", a=2), sums[:, :, :, 0:C],
                                        inv_gam0[:, :, :].unsqueeze(3).to_broadcast([P, 2, BPC // 2, C]),
                                        ALU.mult).then_inc(att0_ready, 1)

            def rebase(value):
                chain.base, chain.n = value, 0

            dve.wait_ge(const_ready, 10)
            with dve.Fori(0, B) as image:
                start = image * PER_IMAGE + START
                rebase(start)
                transposed(image, 0)
                for r in range(1, RND, 2):
                    dve.wait_ge(pj_ps, image * RND + r + 1)
                    nc.vector.tensor_copy(proj[:, r * TR:(r + 1) * TR, 0:PW],
                                          score_banks[:, r % 4, :].rearrange("p (k n) -> p k n", k=TR)[:, :, 0:PW]
                                          ).then_inc(pj_dve, 1)
                dve.wait_ge(pj_dve, (image + 1) * (RND // 2))
                dve.wait_ge(pj_act, (image + 1) * (RND // 2))
                src = proj[:, :, 0:GFW]
                for k in range(3):
                    nc.vector.tensor_copy(piece[k][:, :, :], src).then_inc(piece_ready, 1)
                    if k < 2:
                        dve.wait_ge(piece_ready, image * 3 + k + 1)
                        chain.link(nc.vector.tensor_tensor(rest[k][:, :, :], src, piece[k][:, :, :], ALU.subtract))
                        src = rest[k][:, :, :]
                nc.vector.tensor_reduce(v_abs[:, 0:1], proj[:, :, GFW:PW], mybir.AxisListType.XY, ALU.max,
                                        apply_absolute_value=True).then_inc(v_abs_ready, 1)
                for r in range(NCH):
                    dve.wait_ge(gt_ps, image * NCH + r + 1)
                    nc.vector.tensor_copy(g_tr[0:KS, r * CH:(r + 1) * CH],
                                          score_banks[0:KS, 2 * (r % 2) + 1, :].bitcast(BF16)).then_inc(gt_sb, 1)
                image_scale(image, 0, 0)
                assert chain.n == LINK_PIECES
                with dve.Fori(0, BPC) as blk:
                    block_max(image, blk, blk, range(ATN))
                split_max(image, 0)
                with dve.Fori(0, NCH - 1) as q:
                    rebase(start + LINK_PIECES + LINK_MAX + q * (LINK_MAX + LINK_ATT))
                    steps0(image, q, True)
                    split_max(image, q + 1)
                    attention0(image, q)
                    assert chain.n == LINK_MAX + LINK_ATT
                steps0(image, NCH - 1, False)
                rebase(start + L0 - LINK_ATT)
                attention0(image, NCH - 1)

                rebase(start + L0)
                transposed(image, 1)
                wait_x_tr(dve, image, 1)
                chain.link(nc.vector.tensor_reduce(x_abs[0:C, :], x_tr[0:C, :], AX_X, ALU.max, apply_absolute_value=True))
                nc.vector.tensor_tensor(bound_in[:, :], x_abs[:, :], w_row[:, :], ALU.mult).then_inc(bound_sent, 1)
                dve.wait_ge(bound_ps, image + 1)
                chain.link(nc.vector.tensor_scalar(bound[:, :], sum_banks[:, 0, 0:1], 2.0 ** -100, None, ALU.max))
                chain.link(nc.vector.tensor_scalar(pow2[:, :].bitcast(I32), bound[:, :].bitcast(I32), EXPONENT_BITS,
                                                   None, ALU.bitwise_and))
                chain.link(nc.vector.reciprocal(inv_pow2[:, :], pow2[:, :]))
                chain.link(nc.vector.tensor_scalar(up[:, :], inv_pow2[:, :], 2.0 ** HALF_TOP, None, ALU.mult))
                chain.link(nc.vector.tensor_scalar(down1[:, :], pow2[:, :], 2.0 ** -HALF_TOP, None, ALU.mult))
                chain.link(nc.vector.tensor_tensor(down[:, :], down1[:, :], down1[:, :], ALU.mult))
                chain.link(nc.vector.tensor_scalar(neg_down[:, :], down[:, :], -1.0, None, ALU.mult))
                nc.vector.tensor_scalar(w1s[:, :], w1[:, :, :].rearrange("p a c -> p (a c)"), up[0:C1, 0:1], None,
                                        ALU.mult).then_inc(w1s_ready, 1)
                for c in range(2 * NQ):
                    dve.wait_ge(high_done, image * 2 * NQ + c + 1)
                    cols = slice((c // 2) * BANK, (c // 2 + 1) * BANK)
                    if c % 2 == 0:
                        nc.vector.tensor_tensor(k_low[:, cols], score_banks[:, c % 4, :], k_high[:, cols],
                                                ALU.subtract).then_inc(low_done, 1)
                    else:
                        nc.vector.tensor_tensor(q_split[C:P, cols], score_banks[C:P, c % 4, :], q_split[C:P, cols],
                                                ALU.subtract).then_inc(low_done, 1)

                dve.wait_ge(v1_sb, (image + 1) * NCH)
                nc.vector.tensor_reduce(v_abs[:, 1:2], v1[:, :, :], mybir.AxisListType.XY, ALU.max,
                                        apply_absolute_value=True).then_inc(v_abs_ready, 1)
                image_scale(image, 1, -EXP_UP)
                assert chain.n == LINK_BOUND

                def weigh_chunks(i, par):
                    dve.wait_ge(chunk_w_ready, image * T + i + 1)
                    dve.wait_ge(exp1_done, image * STEPS1 + (i + 1) * NCH + FREE_S1)
                    chain.link(nc.vector.tensor_tensor_reduce(
                        out=part_scr[:, :], in0=part_sum[:, par, :], in1=chunk_w[:, par, :], scale=1.0, scalar=0.0,
                        op0=ALU.mult, op1=ALU.add, accum_out=row_sum1[:, par:par + 1]))
                    chain.link(nc.vector.reciprocal(inv_sum1[:, par:par + 1], row_sum1[:, par:par + 1]))
                    chain.link(nc.vector.tensor_scalar(norm_w[:, par, :], chunk_w[:, par, :], inv_sum1[:, par:par + 1],
                                                       v_up[:, 1:2], ALU.mult, ALU.mult))

                def weigh_values(i, par):
                    dve.wait_ge(pv1_done, image * NCH * T + i * NCH + FREE_E1 - NCH)
                    chain.link(nc.vector.tensor_tensor(v_scaled[:, par, :, :],
                                                       v1[:, i, :].unsqueeze(1).to_broadcast([P, NCH, C]),
                                                       norm_w[:, par, :].unsqueeze(2).to_broadcast([P, NCH, C]), ALU.mult))
                    chain.link(nc.vector.tensor_copy(v_high[:, par, :, :], v_scaled[:, par, :, :]))
                    nc.vector.tensor_tensor(v_low[:, par, :, :], v_scaled[:, par, :, :], v_high[:, par, :, :],
                                            ALU.subtract).then_inc(v_split_ready, 1)

                def steps1(t, first):
                    for u in range(U1):
                        k = image * NCH * T + t * U1 + u
                        par, j = u // NCH, u % NCH
                        dve.wait_ge(s_ready, k + 1)
                        chain.link(nc.vector.reduce_max(chunk_max[:, par, j:j + 1],
                                                        score_banks[:, 2 * (u % 2):2 * (u % 2) + 2, :]
                                                        .rearrange("p a n -> p (a n)"), AX_X))
                        nc.vector.tensor_scalar(exp_bias[:, u:u + 1], chunk_max[:, par, j:j + 1], neg_down[:, 0:1],
                                                LOG_UP, ALU.mult, ALU.add).then_inc(bias_ready, 1)
                        if j == NCH - 1:
                            chain.link(nc.vector.reduce_max(row_max1[:, par:par + 1], chunk_max[:, par, :], AX_X))
                            nc.vector.tensor_scalar(below_max[:, par, :], chunk_max[:, par, :],
                                                    row_max1[:, par:par + 1], down[:, 0:1], ALU.subtract, ALU.mult
                                                    ).then_inc(below_ready, 1)
                        if j < 2 and not (first and u < 2):
                            (weigh_chunks, weigh_values)[j](t * 2 + par - 1, 1 - par)

                main = start + L0 + LINK_BOUND
                rebase(main)
                steps1(0, True)
                with dve.Fori(1, T // 2) as t:
                    rebase(main + t * (2 * LINK_BLOCK) - LINK_W)
                    steps1(t, False)
                    assert chain.n == 2 * LINK_BLOCK
                rebase(start + PER_IMAGE - LINK_W)
                weigh_chunks(T - 1, 1)
                weigh_values(T - 1, 1)
                dve.wait_ge(pv1_done, (image + 1) * NCH * T + FREE_E1)
                dve.wait_ge(y_stored, image * NCH * 16 + 16 * FREE)
                for j in range(NCH):
                    blocks = slice(j * BPC, (j + 1) * BPC)
                    nc.vector.scalar_tensor_tensor(
                        out=y[:, blocks, :].rearrange("p k c -> p (k c)"), in0=sum_banks[:, j, :],
                        scalar=gam_down[:, 1:2], in1=x_mid[:, blocks, :].rearrange("p k c -> p (k c)"),
                        op0=ALU.mult, op1=ALU.add).then_inc(y_ready, 1)


_INS = ['x', 'L0_conv_wf', 'L0_conv_bf', 'L0_conv_wg', 'L0_conv_bg', 'L0_conv_wh', 'L0_conv_bh', 'L0_conv_gamma',
        'L1_conv_Wq', 'L1_conv_bq', 'L1_conv_Wk', 'L1_conv_bk', 'L1_conv_Wv', 'L1_conv_bv', 'L1_conv_gamma']


def kernel(**inputs):
    import numpy as _np
    import concourse.bacc as _bacc
    from concourse import mybir as _mybir
    from concourse.bass_utils import run_bass_kernel_spmd as _run

    nc = _bacc.Bacc("TRN2", target_bir_lowering=False, num_devices=1)
    arrays, args = {}, []
    for name in _INS:
        a = _np.ascontiguousarray(inputs[name])
        arrays[f"in_{name}_dram"] = a
        args.append(nc.dram_tensor(f"in_{name}_dram", a.shape, _mybir.dt.from_np(a.dtype), kind="ExternalInput").ap())
    shape = tuple(inputs['x'].shape)
    args.append(nc.dram_tensor("out_0_dram", shape, _mybir.dt.float32, kind="ExternalOutput").ap())
    attention_pair_kernel(nc, *args)
    r = _run(nc, [arrays], core_ids=[0])
    return r.results[0]["out_0_dram"]
```

```python
import math
from contextlib import ExitStack

import concourse.bass as bass
from concourse import mybir

F32 = mybir.dt.float32
F16 = mybir.dt.float16
BF16 = mybir.dt.bfloat16
I32 = mybir.dt.int32
ALU = mybir.AluOpType
ACT = mybir.ActivationFunctionType
AX_X = mybir.AxisListType.X
ds = bass.ds

P = 128
BANK = 512
EXPONENT_BITS = 0x7F800000
EXP_UP = 15
LOG_UP = EXP_UP * math.log(2.0)
HALF_TOP = 14


def attention_pair_kernel(nc, x, wf, bf, wg, bg, wh, bh, gamma0, wq, bq, wk, bk, wv, bv, gamma1, out):
    B, H, W, C = x.shape
    N = H * W
    CK = wf.shape[1]
    T = N // P
    C1 = C + 1
    NQ = N // BANK
    CH = 2 * BANK
    NCH = N // CH
    BPC = CH // P
    KS = 9 * CK
    KM = KS + 3
    MROW = 64
    GFW = 2 * CK
    PW = GFW + C
    VW = C + 1
    TR = BANK // P
    RND = T // TR
    RT = T // BPC
    ATN = N // BANK
    ATS = T * ATN
    U0 = 8
    U1 = 2 * NCH
    RING = 4
    LAG0 = 5
    LAG1 = 7
    STEPS0, STEPS1 = NCH * T, T * NCH
    HIGH = [{"act": [0, 1, 2], "pool": [3]}, {"act": [0, 1], "pool": [2]}]
    LOW = [{"dve": [0, 1], "pool": [2, 3]}, {"pool": [0, 1, 2]}]
    WHOLE = 3
    DVE_BEHIND = 2
    FREE_ST, FREE_A, FREE_E0, FREE_S1, FREE_E1 = 2, 2, U0, 2, U1
    FREE_LOW = RING
    FREE = 1
    assert N % (P * BPC) == 0 and C == 64 and CK == 8 and NCH == 4

    x_t = x.rearrange("b h w c -> b (h w) c").rearrange("b (p t) c -> b p t c", p=P)
    out_t = out.rearrange("b h w c -> b (h w) c").rearrange("b (p t) c -> b p t c", p=P)

    with ExitStack() as ctx:
        def sb(name, shape, dt):
            return ctx.enter_context(nc.sbuf_tensor(name, shape, dt))

        def sem(name):
            return ctx.enter_context(nc.semaphore(name))

        score_banks = ctx.enter_context(nc.psum_tensor("score_banks", [P, 4, BANK], F32))
        sum_banks = ctx.enter_context(nc.psum_tensor("sum_banks", [P, 4, BANK], F32))

        x_in = sb("x_in", [P, T + BPC, C], F32)
        x_mid = sb("x_mid", [P, T, C], F32)
        x_tr = sb("x_tr", [C1, N], F32)
        w0 = sb("w0", [C1, PW], F32)
        w1 = sb("w1", [C1, 2, C], F32)
        w1s = sb("w1s", [C1, 2 * C], F32)
        w1v = sb("w1v", [C1, C], F32)
        w_row = sb("w_row", [C1, 1], F32)
        x_abs = sb("x_abs", [C1, 1], F32)
        bound_in = sb("bound_in", [C1, 1], F32)
        gammas = sb("gammas", [P, 2], F32)
        ident = sb("ident", [P, P], F32)
        ident_b = sb("ident_b", [P, P], BF16)
        ones = sb("ones", [C1, 1], F32)
        zeros = sb("zeros", [P, P], F16)
        ones_b = sb("ones_b", [P, 1], BF16)
        credit = sb("credit", [P, 13], F32)
        proj = sb("proj", [P, T, PW + 1], F32)
        piece = [sb(f"piece{k}", [P, T, GFW], BF16) for k in range(3)]
        g_stack = sb("g_stack", [P, 2, T, KM + 1], BF16)
        f_stack = sb("f_stack", [P, T, KM + 1], BF16)
        g_tr = sb("g_tr", [KM, 2, N], BF16)
        f_tr = sb("f_tr", [KM, 2, N], BF16)
        tile_max = sb("tile_max", [P, BPC, ATN], F32)
        row_max0 = sb("row_max0", [P, BPC], F32)
        max_rest = sb("max_rest", [P, BPC], F32)
        inv_sum0 = sb("inv_sum0", [P, 2, BPC // 2], F32)
        inv_gam0 = sb("inv_gam0", [P, 2, BPC // 2], F32)
        att0 = sb("att0", [P, BPC, C], F32)
        probs = sb("probs", [P, RING, CH], F32)
        e_high = sb("e_high", [P, U1, CH], F16)
        e_whole = sb("e_whole", [P, U1 // 4, CH], F32)
        e_low = sb("e_low", [P, U1, CH], F16)
        h_high = sb("h_high", [P, 2, T, VW], F16)
        h_low = sb("h_low", [P, 2, T, C], F16)
        v_abs = sb("v_abs", [P, 2], F32)
        v_top = sb("v_top", [P, 2], F32)
        v_top1 = sb("v_top1", [P, 2], F32)
        v_pow2 = sb("v_pow2", [P, 2], F32)
        v_inv = sb("v_inv", [P, 2], F32)
        v_up = sb("v_up", [P, 2], F32)
        gam_down0 = sb("gam_down0", [P, 2], F32)
        gam_down1 = sb("gam_down1", [P, 1], F32)
        q_split = sb("q_split", [P, N], F16)
        k_high = sb("k_high", [P, N], F16)
        k_low = sb("k_low", [P, N], F16)
        v1 = sb("v1", [P, T, C], F32)
        v_scaled = sb("v_scaled", [P, 2, NCH, C], F32)
        v_high = sb("v_high", [P, 2, NCH, C], F16)
        v_low = sb("v_low", [P, 2, NCH, C], F16)
        log_up = sb("log_up", [P, 1], F32)
        bound = sb("bound", [P, 1], F32)
        pow2 = sb("pow2", [P, 1], F32)
        inv_pow2 = sb("inv_pow2", [P, 1], F32)
        up = sb("up", [P, 1], F32)
        down1 = sb("down1", [P, 1], F32)
        down = sb("down", [P, 1], F32)
        neg_down = sb("neg_down", [P, 1], F32)
        chunk_max = sb("chunk_max", [P, 2, NCH], F32)
        exp_bias = sb("exp_bias", [P, U1], F32)
        row_max1 = sb("row_max1", [P, 2], F32)
        below_max = sb("below_max", [P, 2, NCH], F32)
        chunk_w = sb("chunk_w", [P, 2, NCH], F32)
        part_sum = sb("part_sum", [P, 2, NCH], F32)
        part_scr = sb("part_scr", [P, NCH], F32)
        row_sum1 = sb("row_sum1", [P, 2], F32)
        inv_sum1 = sb("inv_sum1", [P, 2], F32)
        norm_w = sb("norm_w", [P, 2, NCH], F32)

        w_in, x_loaded, y_stored = sem("w_in"), sem("x_loaded"), sem("y_stored")
        ident_zero, ident_f, ident_ready, const_ready = sem("ident_zero"), sem("ident_f"), sem("ident_ready"), sem("const_ready")
        w_ready = sem("w_ready")
        xt_ps, xt_act, xt_dve = ([sem(f"{n}_{layer}") for layer in range(2)] for n in ("xt_ps", "xt_act", "xt_dve"))
        pj_ps, pj_act, pj_dve = sem("pj_ps"), sem("pj_act"), sem("pj_dve")
        piece_ready, g_stacked, f_stacked = sem("piece_ready"), sem("g_stacked"), sem("f_stacked")
        ft_ps, gt_ps, ft_sb, gt_sb = sem("ft_ps"), sem("gt_ps"), sem("ft_sb"), sem("gt_sb")
        a_ready, a_used = sem("a_ready"), sem("a_used")
        max_split, mrow_ps, mrow_sb = sem("max_split"), sem("mrow_ps"), sem("mrow_sb")
        st_ready, exp0_done, pv0_done = sem("st_ready"), sem("exp0_done"), sem("pv0_done")
        att0_ready, x_mid_ready = sem("att0_ready"), sem("x_mid_ready")
        bound_sent, bound_ps, w1s_ready = sem("bound_sent"), sem("bound_ps"), sem("w1s_ready")
        v1_ps, v1_sb = sem("v1_ps"), sem("v1_sb")
        qk_ps, high_done, low_done = sem("qk_ps"), sem("high_done"), sem("low_done")
        k_copied = [sem(f"k_copied_{j}") for j in range(NCH)]
        s_ready, bias_ready, exp1_done, pv1_done = sem("s_ready"), sem("bias_ready"), sem("exp1_done"), sem("pv1_done")
        below_ready, chunk_w_ready, y_ready = sem("below_ready"), sem("chunk_w_ready"), sem("y_ready")
        dve_step = sem("dve_step")
        high_by = {"act": sem("high_by_act"), "pool": sem("high_by_pool")}
        low_by = {"dve": sem("low_by_dve"), "pool": sem("low_by_pool")}
        v_abs_ready, v_top_ready = ([sem(f"{n}_{layer}") for layer in range(2)] for n in ("v_abs_ready", "v_top_ready"))
        h_scale_ready = sem("h_scale_ready")
        h_scaled_ready, h_high_ready, h_low_ready = sem("h_scaled_ready"), sem("h_high_ready"), sem("h_low_ready")
        v_split_ready = sem("v_split_ready")
        pool_go = sem("pool_go")

        block = ctx.enter_context(nc.Block())
        N_W = 14

        def wait_x_tr(eng, image, layer):
            eng.wait_ge(xt_act[layer], (image + 1) * RT)
            eng.wait_ge(xt_dve[layer], (image + 1) * RT)

        def loads(image, early=False):
            return image + 1 if early else image * 2

        def half_of_blocks(r, odd):
            return x_tr[0:C, r * CH:(r + 1) * CH].rearrange("c (k a n) -> c k a n", a=2, n=P)[:, :, odd, :]

        def part_done(table, sems, layer, image, k4, u, wraps_back=0):
            by = next(e for e, slots in table[layer].items() if u % 4 in slots)
            n = [len(table[l].get(by, [])) for l in range(2)]
            before = n[0] * STEPS0 // 4 if layer == 1 else 0
            rank = table[layer][by].index(u % 4) + 1
            return sems[by], image * ((n[0] * STEPS0 + n[1] * STEPS1) // 4) + before + (k4 - wraps_back) * n[layer] + rank

        def wait_high(eng, layer, image, k4, u):
            eng.wait_ge(*part_done(HIGH, high_by, layer, image, k4, u))

        def wait_low(eng, layer, image, k4, u, ago=0):
            done, count = part_done(LOW, low_by, layer, image, k4, u, ago)
            eng.wait_ge(done, count + FREE_LOW)

        def split_high(copy, slot, u):
            return copy(e_high[:, slot, :], probs[:, u % RING, :])

        def split_low(subtract, slot, u):
            return subtract(e_low[:, slot, :], probs[:, u % RING, :], e_high[:, slot, :], ALU.subtract)

        @block.sync
        def _(sp):
            def load(image, first_block):
                sp.dma_start(x_in[:, first_block:first_block + T, :], x_t[image]).then_inc(x_loaded, 16)

            for col, w_, b_ in ((0, wg, bg), (CK, wf, bf), (GFW, wh, bh)):
                n = w_.shape[1]
                sp.dma_start(w0[0:C, col:col + n], w_).then_inc(w_in, 16)
                sp.dma_start(w0[C:C1, col:col + n], b_.unsqueeze(0)).then_inc(w_in, 16)
            load(0, 0)
            for k, w_, b_ in ((0, wq, bq), (1, wk, bk)):
                sp.dma_start(w1[0:C, k, :], w_).then_inc(w_in, 16)
                sp.dma_start(w1[C:C1, k, :], b_.unsqueeze(0)).then_inc(w_in, 16)
            sp.dma_start(w1v[0:C, :], wv).then_inc(w_in, 16)
            sp.dma_start(w1v[C:C1, :], bv.unsqueeze(0)).then_inc(w_in, 16)
            sp.dma_start(gammas[:, 0:1], gamma0.partition_broadcast(P)).then_inc(w_in, 16)
            sp.dma_start(gammas[:, 1:2], gamma1.partition_broadcast(P)).then_inc(w_in, 16)

            sp.wait_ge(xt_ps[0], RT)
            load(1 % B, 0)
            sp.wait_ge(xt_ps[0], 2 * RT)
            load(0, BPC)
            with sp.Fori(0, B) as image:
                ahead, following = (image + 2) % B, (image + 1) % B
                sp.wait_ge(x_mid_ready, image * NCH + NCH - 1 + FREE)
                load(ahead, 0)
                sp.wait_ge(xt_ps[1], (image + 1) * RT)
                load(following, BPC)
                for j in range(NCH):
                    cols = slice(j * CH, (j + 1) * CH)
                    for part, done in ((k_high, high_done), (k_low, low_done)):
                        sp.wait_ge(done, 2 * (image * NQ + (j + 1) * (CH // BANK)))
                        sp.dma_start(part[0:C, cols], part[C:P, cols]).then_inc(k_copied[j], 16)
                for j in range(NCH):
                    sp.wait_ge(y_ready, image * NCH + j + 1 + FREE)
                    sp.dma_start(out_t[image, :, j * BPC:(j + 1) * BPC, :],
                                 x_mid[:, j * BPC:(j + 1) * BPC, :]).then_inc(y_stored, 16)
            sp.wait_ge(x_loaded, (3 + 2 * B) * 16)
            sp.wait_ge(y_stored, 16 * (NCH * B + FREE))

        @block.gpsimd
        def _(pool):
            nc.gpsimd.memset(ident[:], 0.0).then_inc(ident_zero, 1)
            pool.wait_ge(ident_zero, 1)
            nc.gpsimd.affine_select(out=ident[:], in_=ident[:], compare_op=ALU.not_equal, fill=1.0, base=0,
                                    pattern=[[-1, P]], channel_multiplier=1).then_inc(ident_f, 1)
            pool.wait_ge(ident_f, 1)
            nc.gpsimd.tensor_copy(ident_b[:], ident[:]).then_inc(ident_ready, 1)
            nc.gpsimd.memset(g_stack[:], 0.0).then_inc(const_ready, 1)
            nc.gpsimd.memset(f_stack[:], 1.0).then_inc(const_ready, 1)
            nc.gpsimd.memset(proj[:, :, PW:PW + 1], 1.0).then_inc(const_ready, 1)
            nc.gpsimd.memset(ones[:], 1.0).then_inc(const_ready, 1)
            nc.gpsimd.memset(ones_b[:], 1.0).then_inc(const_ready, 1)
            nc.gpsimd.memset(credit[:, 0:1], 0.0).then_inc(exp0_done, FREE_ST)
            nc.gpsimd.memset(credit[:, 1:2], 0.0).then_inc(a_used, FREE_A)
            nc.gpsimd.memset(credit[:, 2:3], 0.0).then_inc(pv0_done, FREE_E0)
            nc.gpsimd.memset(credit[:, 3:4], 0.0).then_inc(exp1_done, FREE_S1)
            nc.gpsimd.memset(credit[:, 4:5], 0.0).then_inc(pv1_done, FREE_E1)
            nc.gpsimd.memset(credit[:, 5:6], 0.0).then_inc(low_by["pool"], FREE_LOW)
            nc.gpsimd.memset(credit[:, 6:7], 0.0).then_inc(low_by["dve"], FREE_LOW)
            nc.gpsimd.memset(log_up[:], LOG_UP).then_inc(const_ready, 1)
            for n, (free, by) in enumerate(((y_ready, FREE), (att0_ready, FREE), (x_mid_ready, FREE), (y_stored, 16 * FREE),
                                               (h_low_ready, FREE))):
                nc.gpsimd.memset(credit[:, 8 + n:9 + n], 0.0).then_inc(free, by)
            nc.gpsimd.memset(zeros[:], 0.0).then_inc(const_ready, 1)
            nc.gpsimd.memset(h_high[:, :, :, C:VW], 1.0).then_inc(const_ready, 1)
            pool.wait_ge(const_ready, 10)

            def largest_value(image, layer):
                pool.wait_ge(v_abs_ready[layer], image + 1)
                pool.sem_inc(pool_go, 1)
                nc.gpsimd.partition_all_reduce(v_top[:, layer:layer + 1], v_abs[:, layer:layer + 1], P,
                                               bass.bass_isa.ReduceOp.max).then_inc(v_top_ready[layer], 1)

            def split(layer, image, k, k4, u, slot):
                high, low = u % 4 in HIGH[layer]["pool"], u % 4 in LOW[layer]["pool"]
                step = image * STEPS0 + k
                if high:
                    pool.wait_ge(*((exp0_done, step + 1 + FREE_ST) if layer == 0 else (exp1_done, step + 1 + FREE_S1)))
                    pool.wait_ge(pv0_done if layer == 0 else pv1_done, step + 1)
                    pool.sem_inc(pool_go, 1)
                    split_high(lambda o, i: nc.gpsimd.tensor_scalar(o, i, 1.0, 0.0, ALU.mult, ALU.add), slot, u
                               ).then_inc(high_by["pool"], 1)
                if low:
                    wait_high(pool, layer, image, k4, u)
                    split_low(nc.gpsimd.tensor_tensor, slot, u).then_inc(low_by["pool"], 1)

            def steps1(image, t):
                for u in range(U1):
                    split(1, image, t * U1 + u, t * 2 + u // 4, u, u)

            def stack_g(image, par):
                for k in range(3):
                    pool.wait_ge(piece_ready, image * 3 + k + 1)
                    dst = g_stack[:, par, :, 3 * CK * k:3 * CK * (k + 1)].rearrange("p t (r c) -> p t r c", r=3)
                    src = piece[k][:, :, 0:CK].unsqueeze(2).to_broadcast([P, T, 3, CK])
                    one = ones_b[:, :].unsqueeze(2).unsqueeze(3).to_broadcast([P, T, 3, CK])
                    nc.gpsimd.tensor_tensor(dst, src, one, ALU.mult).then_inc(g_stacked, 1)

            def low_values(image, par, r):
                blocks = slice(r * BPC, (r + 1) * BPC)
                pool.wait_ge(h_high_ready, image * NCH + r + 1)
                nc.gpsimd.tensor_tensor(h_low[:, par, blocks, :], proj[:, blocks, GFW:PW],
                                        h_high[:, par, blocks, 0:C], ALU.subtract).then_inc(h_low_ready, 1)

            with pool.Fori(0, 2) as image:
                stack_g(image, image % 2)
                largest_value(image, 0)
                for r in range(NCH):
                    low_values(image, image % 2, r)
            with pool.Fori(0, B) as image:
                with pool.Fori(0, NCH) as q:
                    with pool.Fori(0, T // U0) as t:
                        for u in range(U0):
                            split(0, image, q * T + t * U0 + u, q * (T // 4) + t * (U0 // 4) + u // 4, u, u)
                    pool.wait_ge(x_loaded, 16 * (2 * image + 3))
                    pool.wait_ge(y_stored, (image * NCH + FREE) * 16)
                    pool.wait_ge(att0_ready, image * NCH + q + 1 + FREE)
                    nc.gpsimd.tensor_tensor(x_mid[:, ds(q * BPC, BPC), :], att0[:, :, :],
                                            x_in[:, ds(q * BPC + BPC, BPC), :], ALU.add).then_inc(x_mid_ready, 1)
                par = image % 2
                stack_g(image + 2, par)
                largest_value(image + 2, 0)
                largest_value(image, 1)
                for r in range(NCH):
                    low_values(image + 2, par, r)
                with pool.Fori(0, T // 2) as t:
                    steps1(image, t)

        @block.tensor
        def _(pe):
            def transposes(image, layer, src):
                for r in range(RT):
                    if layer == 1:
                        pe.wait_ge(x_mid_ready, image * NCH + r + 1 + FREE)
                    for k in range(BPC // 2):
                        t = r * BPC + 2 * k
                        mm = nc.tensor.transpose(score_banks[:, r, k * P:(k + 1) * P],
                                                 src[:, t:t + 2, :].rearrange("p a c -> p (a c)"), ident[:, :])
                    mm.then_inc(xt_ps[layer], 1)

            def project0(image, early):
                pe.wait_ge(x_loaded, 16 * loads(image, early))
                transposes(image, 0, x_in)
                wait_x_tr(pe, image, 0)
                pe.wait_ge(h_low_ready, image * NCH + FREE)
                for r in range(RND):
                    if r >= 4:
                        pe.wait_ge(pj_act if r % 2 == 0 else pj_dve, image * (RND // 2) + (r - 4) // 2 + 1)
                    for k in range(TR):
                        t = r * TR + k
                        mm = nc.tensor.matmul(score_banks[:, r % 4, k * P:k * P + PW], x_tr[:, t * P:(t + 1) * P],
                                              w0[:, :], start=True, stop=True)
                    mm.then_inc(pj_ps, 1)
                pe.wait_ge(pj_act, (image + 1) * (RND // 2))
                pe.wait_ge(pj_dve, (image + 1) * (RND // 2))

            def transpose_stacks(image, par, rounds=range(NCH)):
                for r in rounds:
                    for src, stacked, used, ready, which in ((f_stack, f_stacked, ft_sb, ft_ps, 0),
                                                             (g_stack, g_stacked, gt_sb, gt_ps, 1)):
                        if r == 0:
                            pe.wait_ge(stacked, (image + 1) * 3)
                        if r >= 2:
                            pe.wait_ge(used, image * NCH + r - 1)
                        bank = sum_banks[0:KM, 2 * (r % 2) + which, :].bitcast(BF16)
                        rows = KM if which == 0 else KS
                        for k in range(BPC):
                            t = r * BPC + k
                            blk = src[:, t, 0:rows] if which == 0 else src[:, par, t, 0:rows]
                            mm = nc.tensor.transpose(bank[0:rows, k * P:(k + 1) * P], blk, ident_b[:, :])
                        mm.then_inc(ready, 1)

            def max_pass_tile(image, par, blk, j):
                tile = image * ATS + blk * ATN + j
                pe.wait_ge(a_used, tile + 1)
                nc.tensor.matmul(sum_banks[:, 2 + j % 2, :], g_tr[0:KS, par, ds(blk * P, P)],
                                 f_tr[0:KS, par, j * BANK:(j + 1) * BANK], start=True, stop=True).then_inc(a_ready, 1)

            def max_rows(image, par, q):
                pe.wait_ge(max_split, image * NCH + q + 1)
                for k in range(BPC):
                    mm = nc.tensor.matmul(sum_banks[0:KM, 2 + k // 4, (k % 4) * P:(k % 4 + 1) * P],
                                          g_stack[:, par, q * BPC + k, 0:KM], ident_b[:, :], start=True, stop=True)
                mm.then_inc(mrow_ps, 1)

            def scores0(image, par, q, i, u):
                step = image * NCH * T + q * T + i
                pe.wait_ge(exp0_done, step + 1)
                for h in range(2):
                    mm = nc.tensor.matmul(score_banks[:, 2 * (u % 2) + h, :], f_tr[0:KM, par, ds(i * P, P)],
                                          g_tr[0:KM, par, ds(q * CH + h * BANK, BANK)], start=True, stop=True)
                mm.then_inc(st_ready, 1)

            def products(low_slot, bank_of, width, pitch, highs, lows):
                for n in range(BPC):
                    bank, o = bank_of(n)
                    for e in (e_high, e_low):
                        for v in (highs, lows):
                            mm = nc.tensor.matmul(sum_banks[:, bank, o:o + v.shape[-1]], e[:, low_slot, n * P:(n + 1) * P],
                                                  v, start=False, stop=True, skip_group_check=True)
                return mm

            def open_sums(banks):
                for j in range(banks):
                    nc.tensor.matmul(sum_banks[:, j, :], zeros[:, :],
                                     zeros[:, :].unsqueeze(1).to_broadcast([P, BANK // P, P]), start=True, stop=True,
                                     skip_group_check=True)

            def values0(image, par, q, i, k4, u):
                wait_low(pe, 0, image, k4, u)
                products(u % U0, lambda n: (n // 4, (n % 4) * VW), VW, VW,
                         h_high[:, par, i, :], h_low[:, par, i, :]).then_inc(pv0_done, 1)

            def chunk0(image, par, q, ahead):
                pe.wait_ge(exp1_done, image * STEPS1 + FREE_S1)
                pe.wait_ge(mrow_sb, image * NCH + q + 1)

                def steps(t, first):
                    for u in range(U0):
                        i = t * U0 + u
                        scores0(image, par, q, i, u)
                        if first and u == 0:
                            pe.wait_ge(y_ready, image * NCH + FREE)
                        for j in range(2 * (u % 4), 2 * (u % 4) + 2):
                            max_pass_tile(*ahead[:2], ahead[2] * BPC + t * (U0 // 4) + u // 4, j)
                        if first and u == LAG0:
                            pe.wait_ge(att0_ready, image * NCH + q + FREE)
                            pe.wait_ge(h_low_ready, (image + 1) * NCH + FREE)
                            open_sums(2)
                        if not first or u >= LAG0:
                            values0(image, par, q, i - LAG0, q * (T // 4) + t * (U0 // 4) + (u - LAG0) // 4, u - LAG0)

                steps(0, True)
                with pe.Fori(1, T // U0) as t:
                    steps(t, False)
                for i in range(T - LAG0, T):
                    values0(image, par, q, i, q * (T // 4) + i // 4, i)
                    if i == T - LAG0 + 1:
                        max_rows(*ahead)

            def scores1(image, i, k, u):
                pe.wait_ge(exp1_done, image * STEPS1 + k + 1)
                for h in range(2):
                    col = (u % NCH) * CH + h * BANK
                    bank = score_banks[:, 2 * (u % 2) + h, :]
                    nc.tensor.matmul(bank, q_split[:, ds(i * P, P)], k_high[:, col:col + BANK], start=True, stop=False)
                    mm = nc.tensor.matmul(bank, q_split[:, ds(i * P, P)], k_low[:, col:col + BANK],
                                          start=False, stop=True)
                mm.then_inc(s_ready, 1)

            def values1(image, i, k4, u):
                u, j = u % U1, u % NCH
                if j == 0:
                    pe.wait_ge(v_split_ready, image * T + i + 1)
                if j == WHOLE:
                    pe.wait_ge(exp1_done, image * STEPS1 + k4 * 4 + j + 1 + FREE_S1)
                    for n in range(BPC):
                        mm = nc.tensor.matmul(sum_banks[:, j, n * C:(n + 1) * C], e_whole[:, u // 4, n * P:(n + 1) * P],
                                              v_scaled[:, u // NCH, j, :], start=False, stop=True,
                                              skip_group_check=True)
                    mm.then_inc(pv1_done, 1)
                    return
                wait_low(pe, 1, image, k4, u)
                products(u, lambda n: (j, n * C), C, C, v_high[:, u // NCH, j, :],
                         v_low[:, u // NCH, j, :]).then_inc(pv1_done, 1)

            pe.wait_ge(ident_ready, 1)
            pe.wait_ge(const_ready, 10)
            pe.wait_ge(w_in, 16 * N_W)
            with pe.Fori(0, 2) as image:
                project0(image, True)
                transpose_stacks(image, image % 2)
                pe.wait_ge(ft_sb, (image + 1) * NCH)
                pe.wait_ge(gt_sb, (image + 1) * NCH)
            with pe.Fori(0, BPC) as blk:
                for j in range(ATN):
                    max_pass_tile(0, 0, blk, j)
            max_rows(0, 0, 0)
            with pe.Fori(0, B) as image:
                par, next_par = image % 2, (image + 1) % 2
                with pe.Fori(0, NCH - 1) as q:
                    chunk0(image, par, q, (image, par, q + 1))
                chunk0(image, par, NCH - 1, (image + 1, next_par, 0))
                pe.wait_ge(exp0_done, (image + 1) * NCH * T + FREE_ST)
                project0(image + 2, False)
                transposes(image, 1, x_mid)
                wait_x_tr(pe, image, 1)
                for r in range(NCH):
                    for k in range(BPC):
                        t = r * BPC + k
                        mm = nc.tensor.matmul(score_banks[:, r, k * C:(k + 1) * C], x_tr[:, t * P:(t + 1) * P],
                                              w1v[:, :], start=True, stop=True)
                    mm.then_inc(v1_ps, 1)
                pe.wait_ge(bound_sent, image + 1)
                nc.tensor.matmul(sum_banks[:, 0, 0:1], bound_in[:, :].to_broadcast([C1, P]), ones[:, :],
                                 start=True, stop=True).then_inc(bound_ps, 1)
                pe.wait_ge(w1s_ready, image + 1)
                pe.wait_ge(mrow_sb, (image + 1) * NCH + 1)
                pe.wait_ge(att0_ready, (image + 1) * NCH + FREE)
                for c in range(NQ):
                    if c < 4:
                        pe.wait_ge(v1_sb, image * NCH + c + 1)
                    else:
                        pe.wait_ge(low_done, 2 * (image * NQ + c - 3))
                    nc.tensor.matmul(score_banks[:, c % 4, :], w1s[:, :], x_tr[:, c * BANK:(c + 1) * BANK],
                                     start=True, stop=True).then_inc(qk_ps, 1)
                    if c % 2 == 1:
                        transpose_stacks(image + 2, par, [c // 2])
                pe.wait_ge(low_done, 2 * (image + 1) * NQ)


                def steps1(t, first):
                    for u in range(U1):
                        if first and u < NCH:
                            pe.wait_ge(k_copied[u], 32 * (image + 1))
                        scores1(image, t * 2 + u // NCH, t * U1 + u, u)
                        if first and u == LAG1:
                            pe.wait_ge(ft_sb, (image + 3) * NCH)
                            pe.wait_ge(gt_sb, (image + 3) * NCH)
                            open_sums(NCH)
                        if not first or u >= LAG1:
                            v = u - LAG1
                            values1(image, t * 2 + v // NCH, t * 2 + v // NCH, v)

                steps1(0, True)
                with pe.Fori(1, T // 2) as t:
                    steps1(t, False)
                for k in range(T * NCH - LAG1, T * NCH):
                    values1(image, k // NCH, k // NCH, k)

        @block.scalar
        def _(act):
            def transposed(image, layer):
                for r in range(RT):
                    act.wait_ge(xt_ps[layer], image * RT + r + 1)
                    nc.scalar.copy(half_of_blocks(r, 0), score_banks[0:C, r, :].rearrange("c (k n) -> c k n", n=P)
                                   ).then_inc(xt_act[layer], 1)

            def max_rows(image, par, q):
                act.wait_ge(mrow_ps, image * NCH + q + 1)
                nc.scalar.copy(g_tr[MROW:KM, par, ds(q * CH, CH)].rearrange("p (a n) -> p a n", a=2),
                               sum_banks[MROW:KM, 2:4, :]).then_inc(mrow_sb, 1)

            def chunk0(image, q, ahead):
                with act.Fori(0, T // U0) as t:
                    for u in range(U0):
                        step = image * NCH * T + q * T + t * U0 + u
                        k4 = q * (T // 4) + t * (U0 // 4) + u // 4
                        act.wait_ge(st_ready, step + 1)
                        wait_low(act, 0, image, k4, u, ago=1)
                        nc.scalar.activation(probs[:, u % RING, :].rearrange("p (a n) -> p a n", a=2),
                                             score_banks[:, 2 * (u % 2):2 * (u % 2) + 2, :],
                                             ACT.Exp, bias=log_up[:, 0:1]).then_inc(exp0_done, 1)
                        if u % 4 in HIGH[0]["act"]:
                            act.wait_ge(exp0_done, step + 1 + FREE_ST)
                            act.wait_ge(pv0_done, step + 1)
                            split_high(nc.scalar.copy, u, u).then_inc(high_by["act"], 1)
                max_rows(*ahead)

            def project0(image):
                transposed(image, 0)
                for r in range(0, RND, 2):
                    act.wait_ge(pj_ps, image * RND + r + 1)
                    nc.scalar.copy(proj[:, r * TR:(r + 1) * TR, 0:PW],
                                   score_banks[:, r % 4, :].rearrange("p (k n) -> p k n", k=TR)[:, :, 0:PW]
                                   ).then_inc(pj_act, 1)

            def stack_f(image):
                for k in range(3):
                    act.wait_ge(piece_ready, image * 3 + k + 1)
                    dst = f_stack[:, :, 0:KS].rearrange("p t (r k c) -> p t r k c", r=3, k=3)[:, :, :, k, :]
                    src = piece[k][:, :, CK:GFW].unsqueeze(2).to_broadcast([P, T, 3, CK])
                    nc.scalar.copy(dst, src).then_inc(f_stacked, 1)

            def transposed_f(image, par, rounds=range(NCH)):
                for r in rounds:
                    act.wait_ge(ft_ps, image * NCH + r + 1)
                    nc.scalar.copy(f_tr[0:KM, par, r * CH:(r + 1) * CH],
                                   sum_banks[0:KM, 2 * (r % 2), :].bitcast(BF16)).then_inc(ft_sb, 1)

            def scale_values(image, r):
                blocks = slice(r * BPC, (r + 1) * BPC)
                act.wait_ge(h_scale_ready, image + 1)
                nc.scalar.activation(proj[:, blocks, GFW:PW], proj[:, blocks, GFW:PW], ACT.Copy,
                                     scale=v_up[:, 0:1]).then_inc(h_scaled_ready, 1)

            def high_values(image, par, r):
                blocks = slice(r * BPC, (r + 1) * BPC)
                act.wait_ge(h_scaled_ready, image * NCH + r + 1)
                nc.scalar.copy(h_high[:, par, blocks, 0:C], proj[:, blocks, GFW:PW]).then_inc(h_high_ready, 1)

            act.wait_ge(const_ready, 10)
            with act.Fori(0, 2) as image:
                project0(image)
                stack_f(image)
                transposed_f(image, image % 2)
                for r in range(NCH):
                    scale_values(image, r)
                for r in range(NCH):
                    high_values(image, image % 2, r)
            max_rows(0, 0, 0)
            with act.Fori(0, B) as image:
                par, next_par = image % 2, (image + 1) % 2
                with act.Fori(0, NCH - 1) as q:
                    chunk0(image, q, (image, par, q + 1))
                chunk0(image, NCH - 1, (image + 1, next_par, 0))

                project0(image + 2)
                transposed(image, 1)
                stack_f(image + 2)
                for r in range(NCH):
                    act.wait_ge(v1_ps, image * NCH + r + 1)
                    nc.scalar.copy(v1[:, r * BPC:(r + 1) * BPC, :],
                                   score_banks[:, r, :].rearrange("p (k c) -> p k c", k=BPC)).then_inc(v1_sb, 1)
                for c in range(NQ):
                    act.wait_ge(qk_ps, image * NQ + c + 1)
                    for dst, rows in ((q_split, slice(0, C)), (k_high, slice(C, P))):
                        nc.scalar.copy(dst[rows, c * BANK:(c + 1) * BANK], score_banks[rows, c % 4, :]
                                       ).then_inc(high_done, 1)
                    if c % 2 == 0:
                        scale_values(image + 2, c // 2)
                    else:
                        transposed_f(image + 2, par, [c // 2])
                        high_values(image + 2, par, c // 2)
                with act.Fori(0, T // 2) as t:
                    for u in range(U1):
                        step = image * STEPS1 + t * U1 + u
                        k4 = t * 2 + u // 4
                        act.wait_ge(bias_ready, step + 1)
                        if u % 4 == WHOLE:
                            act.wait_ge(pv1_done, step + 1)
                            dst = e_whole[:, u // 4, :]
                        else:
                            wait_low(act, 1, image, k4, u, ago=1)
                            dst = probs[:, u % RING, :]
                        nc.scalar.activation(dst.rearrange("p (a n) -> p a n", a=2),
                                             score_banks[:, 2 * (u % 2):2 * (u % 2) + 2, :],
                                             ACT.Exp, bias=exp_bias[:, u:u + 1], scale=down[:, 0:1],
                                             accum_out=part_sum[:, u // NCH, u % NCH:u % NCH + 1]
                                             ).then_inc(exp1_done, 1)
                        if u % 4 in HIGH[1]["act"]:
                            act.wait_ge(exp1_done, step + 1 + FREE_S1)
                            act.wait_ge(pv1_done, step + 1)
                            split_high(nc.scalar.copy, u, u).then_inc(high_by["act"], 1)
                        if u % NCH == NCH - 1:
                            par = u // NCH
                            act.wait_ge(below_ready, image * T + t * 2 + par + 1)
                            nc.scalar.activation(chunk_w[:, par, :], below_max[:, par, :], ACT.Exp
                                                 ).then_inc(chunk_w_ready, 1)

        @block.vector
        def _(dve):
            class Chain:
                base, n = 0, 0

                def link(self, ins):
                    ins.then_inc(dve_step, 1)
                    self.n += 1
                    dve.wait_ge(dve_step, self.base + self.n)

            chain = Chain()

            nc.vector.memset(x_tr[C:C1, :], 1.0).then_inc(const_ready, 1)
            nc.vector.memset(x_abs[C:C1, :], 1.0).then_inc(const_ready, 1)
            dve.wait_ge(w_in, 16 * N_W)
            chain.link(nc.vector.tensor_reduce(w_row[:, :], w1[:, :, :], mybir.AxisListType.XY, ALU.add,
                                               apply_absolute_value=True))
            START = chain.n

            LINK_PIECES, LINK_MAX, LINK_ATT = 6, 4, 2
            LINK_BOUND, LINK_CHUNK, LINK_BELOW, LINK_W = 13, 1, 1, 5
            LINK_BLOCK = NCH * LINK_CHUNK + LINK_BELOW + LINK_W
            L0 = NCH * (LINK_MAX + LINK_ATT)
            BETWEEN = LINK_PIECES + LINK_BOUND
            PER_IMAGE = L0 + BETWEEN + T * LINK_BLOCK

            def transposed(image, layer):
                for r in range(RT):
                    dve.wait_ge(xt_ps[layer], image * RT + r + 1)
                    nc.vector.tensor_copy(half_of_blocks(r, 1), score_banks[C:P, r, :]
                                          .rearrange("c (k n) -> c k n", n=P)).then_inc(xt_dve[layer], 1)

            def block_max(image, blk, slot, js):
                for j in js:
                    dve.wait_ge(a_ready, image * ATS + blk * ATN + j + 1)
                    nc.vector.reduce_max(tile_max[:, slot, j:j + 1], sum_banks[:, 2 + j % 2, :], AX_X
                                         ).then_inc(a_used, 1)

            def steps0(image, q, ahead):
                with dve.Fori(0, T // U0) as t:
                    for u in range(U0):
                        slot = t * (U0 // 4) + u // 4
                        block_max(ahead[0], ahead[2] * BPC + slot, slot, range(2 * (u % 4), 2 * (u % 4) + 2))
                        if (u - DVE_BEHIND) % 4 in LOW[0]["dve"]:
                            low0(image, q * (T // 4) + t * (U0 // 4) + (u - DVE_BEHIND) // 4, u - DVE_BEHIND)

            def low0(image, k4, u):
                wait_high(dve, 0, image, k4, u)
                split_low(nc.vector.tensor_tensor, u, u).then_inc(low_by["dve"], 1)

            def image_scale(image, layer, extra, gam_down):
                col = slice(layer, layer + 1)
                dve.wait_ge(v_top_ready[layer], image + 1)
                chain.link(nc.vector.tensor_scalar(v_top1[:, col], v_top[:, col], 2.0 ** -100, None, ALU.max))
                chain.link(nc.vector.tensor_scalar(v_pow2[:, col].bitcast(I32), v_top1[:, col].bitcast(I32),
                                                   EXPONENT_BITS, None, ALU.bitwise_and))
                chain.link(nc.vector.reciprocal(v_inv[:, col], v_pow2[:, col]))
                chain.link(nc.vector.tensor_scalar(gam_down, v_pow2[:, col], gammas[:, col],
                                                   2.0 ** (extra - HALF_TOP), ALU.mult, ALU.mult))
                up_ = nc.vector.tensor_scalar(v_up[:, col], v_inv[:, col], 2.0 ** (HALF_TOP - extra), None, ALU.mult)
                if layer == 0:
                    up_.then_inc(h_scale_ready, 1)
                else:
                    chain.link(up_)

            def split_max(image, par, q):
                dve.wait_ge(a_used, image * ATS + (q + 1) * BPC * ATN + FREE_A)
                blocks = ds(q * BPC, BPC)
                chain.link(nc.vector.reduce_max(row_max0[:, :], tile_max[:, :, :], AX_X))
                chain.link(nc.vector.tensor_scalar(g_stack[:, par, blocks, KS], row_max0[:, :], -1.0, None, ALU.mult))
                chain.link(nc.vector.scalar_tensor_tensor(max_rest[:, :], row_max0[:, :], -1.0,
                                                          g_stack[:, par, blocks, KS], ALU.mult, ALU.subtract))
                chain.link(nc.vector.tensor_copy(g_stack[:, par, blocks, KS + 1], max_rest[:, :]))
                nc.vector.tensor_tensor(g_stack[:, par, blocks, KS + 2], max_rest[:, :], g_stack[:, par, blocks, KS + 1],
                                        ALU.subtract).then_inc(max_split, 1)

            def attention0(image, par, q):
                dve.wait_ge(pv0_done, image * NCH * T + (q + 1) * T + FREE_E0)
                dve.wait_ge(x_mid_ready, image * NCH + q + FREE)
                sums = sum_banks[:, 0:2, 0:4 * VW].rearrange("p a (k c) -> p a k c", c=VW)
                chain.link(nc.vector.reciprocal(inv_sum0[:, :, :], sums[:, :, :, C]))
                chain.link(nc.vector.tensor_scalar(inv_gam0[:, :, :], inv_sum0[:, :, :], gam_down0[:, ds(par, 1)], None, ALU.mult))
                nc.vector.tensor_tensor(att0[:, :, :].rearrange("p (a k) c -> p a k c", a=2), sums[:, :, :, 0:C],
                                        inv_gam0[:, :, :].unsqueeze(3).to_broadcast([P, 2, BPC // 2, C]),
                                        ALU.mult).then_inc(att0_ready, 1)

            def rebase(value):
                chain.base, chain.n = value, 0

            def project0(image):
                transposed(image, 0)
                for r in range(1, RND, 2):
                    dve.wait_ge(pj_ps, image * RND + r + 1)
                    nc.vector.tensor_copy(proj[:, r * TR:(r + 1) * TR, 0:PW],
                                          score_banks[:, r % 4, :].rearrange("p (k n) -> p k n", k=TR)[:, :, 0:PW]
                                          ).then_inc(pj_dve, 1)

            def pieces(image):
                dve.wait_ge(pj_dve, (image + 1) * (RND // 2))
                dve.wait_ge(pj_act, (image + 1) * (RND // 2))
                src = proj[:, :, 0:GFW]
                for k in range(3):
                    nc.vector.tensor_copy(piece[k][:, :, :], src).then_inc(piece_ready, 1)
                    if k < 2:
                        dve.wait_ge(piece_ready, image * 3 + k + 1)
                        chain.link(nc.vector.tensor_tensor(src, src, piece[k][:, :, :], ALU.subtract))

            def largest_h():
                nc.vector.tensor_reduce(v_abs[:, 0:1], proj[:, :, GFW:PW], mybir.AxisListType.XY, ALU.max,
                                        apply_absolute_value=True).then_inc(v_abs_ready[0], 1)

            def transposed_g(image, par, rounds=range(NCH)):
                for r in rounds:
                    dve.wait_ge(gt_ps, image * NCH + r + 1)
                    nc.vector.tensor_copy(g_tr[0:KS, par, r * CH:(r + 1) * CH],
                                          sum_banks[0:KS, 2 * (r % 2) + 1, :].bitcast(BF16)).then_inc(gt_sb, 1)

            dve.wait_ge(const_ready, 10)
            with dve.Fori(0, 2) as image:
                rebase(image * LINK_PIECES + START)
                project0(image)
                pieces(image)
                largest_h()
                transposed_g(image, image % 2)
                image_scale(image, 0, 0, gam_down0[:, ds(image, 1)])
                assert chain.n == LINK_PIECES
            rebase(START + 2 * LINK_PIECES)
            with dve.Fori(0, BPC) as blk:
                block_max(0, blk, blk, range(ATN))
            split_max(0, 0, 0)
            START += 2 * LINK_PIECES + LINK_MAX
            with dve.Fori(0, B) as image:
                start = image * PER_IMAGE + START
                par, next_par = image % 2, (image + 1) % 2
                with dve.Fori(0, NCH - 1) as q:
                    rebase(start + q * (LINK_MAX + LINK_ATT))
                    steps0(image, q, (image, par, q + 1))
                    split_max(image, par, q + 1)
                    attention0(image, par, q)
                    assert chain.n == LINK_MAX + LINK_ATT
                rebase(start + L0 - LINK_MAX - LINK_ATT)
                steps0(image, NCH - 1, (image + 1, next_par, 0))
                split_max(image + 1, next_par, 0)
                attention0(image, par, NCH - 1)

                rebase(start + L0)
                project0(image + 2)
                pieces(image + 2)
                transposed(image, 1)
                wait_x_tr(dve, image, 1)
                chain.link(nc.vector.tensor_reduce(x_abs[0:C, :], x_tr[0:C, :], AX_X, ALU.max, apply_absolute_value=True))
                nc.vector.tensor_tensor(bound_in[:, :], x_abs[:, :], w_row[:, :], ALU.mult).then_inc(bound_sent, 1)
                largest_h()
                image_scale(image + 2, 0, 0, gam_down0[:, ds(par, 1)])
                dve.wait_ge(bound_ps, image + 1)
                chain.link(nc.vector.tensor_scalar(bound[:, :], sum_banks[:, 0, 0:1], 2.0 ** -100, None, ALU.max))
                chain.link(nc.vector.tensor_scalar(pow2[:, :].bitcast(I32), bound[:, :].bitcast(I32), EXPONENT_BITS,
                                                   None, ALU.bitwise_and))
                chain.link(nc.vector.reciprocal(inv_pow2[:, :], pow2[:, :]))
                chain.link(nc.vector.tensor_scalar(up[:, :], inv_pow2[:, :], 2.0 ** HALF_TOP, None, ALU.mult))
                chain.link(nc.vector.tensor_scalar(down1[:, :], pow2[:, :], 2.0 ** -HALF_TOP, None, ALU.mult))
                chain.link(nc.vector.tensor_tensor(down[:, :], down1[:, :], down1[:, :], ALU.mult))
                chain.link(nc.vector.tensor_scalar(neg_down[:, :], down[:, :], -1.0, None, ALU.mult))
                nc.vector.tensor_scalar(w1s[:, :], w1[:, :, :].rearrange("p a c -> p (a c)"), up[0:C1, 0:1], None,
                                        ALU.mult).then_inc(w1s_ready, 1)
                dve.wait_ge(v1_sb, (image + 1) * NCH)
                nc.vector.tensor_reduce(v_abs[:, 1:2], v1[:, :, :], mybir.AxisListType.XY, ALU.max,
                                        apply_absolute_value=True).then_inc(v_abs_ready[1], 1)
                for c in range(NQ):
                    dve.wait_ge(high_done, 2 * (image * NQ + c + 1))
                    cols = slice(c * BANK, (c + 1) * BANK)
                    nc.vector.tensor_tensor(q_split[C:P, cols], score_banks[0:C, c % 4, :], q_split[0:C, cols],
                                            ALU.subtract).then_inc(low_done, 1)
                    nc.vector.tensor_tensor(k_low[C:P, cols], score_banks[C:P, c % 4, :], k_high[C:P, cols],
                                            ALU.subtract).then_inc(low_done, 1)
                    if c % 2 == 1:
                        transposed_g(image + 2, par, [c // 2])
                image_scale(image, 1, -EXP_UP, gam_down1[:, :])
                assert chain.n == BETWEEN

                def weigh_chunks(i, par):
                    dve.wait_ge(chunk_w_ready, image * T + i + 1)
                    dve.wait_ge(exp1_done, image * STEPS1 + (i + 1) * NCH + FREE_S1)
                    chain.link(nc.vector.tensor_tensor_reduce(
                        out=part_scr[:, :], in0=part_sum[:, par, :], in1=chunk_w[:, par, :], scale=1.0, scalar=0.0,
                        op0=ALU.mult, op1=ALU.add, accum_out=row_sum1[:, par:par + 1]))
                    chain.link(nc.vector.reciprocal(inv_sum1[:, par:par + 1], row_sum1[:, par:par + 1]))
                    chain.link(nc.vector.tensor_scalar(norm_w[:, par, :], chunk_w[:, par, :], inv_sum1[:, par:par + 1],
                                                       v_up[:, 1:2], ALU.mult, ALU.mult))

                def weigh_values(i, par):
                    dve.wait_ge(pv1_done, image * NCH * T + i * NCH + FREE_E1 - NCH)
                    chain.link(nc.vector.tensor_tensor(v_scaled[:, par, :, :],
                                                       v1[:, i, :].unsqueeze(1).to_broadcast([P, NCH, C]),
                                                       norm_w[:, par, :].unsqueeze(2).to_broadcast([P, NCH, C]), ALU.mult))

                def split_values(par):
                    chain.link(nc.vector.tensor_copy(v_high[:, par, :, :], v_scaled[:, par, :, :]))
                    nc.vector.tensor_tensor(v_low[:, par, :, :], v_scaled[:, par, :, :], v_high[:, par, :, :],
                                            ALU.subtract).then_inc(v_split_ready, 1)

                def steps1(t, first):
                    for u in range(U1):
                        k = image * NCH * T + t * U1 + u
                        par, j = u // NCH, u % NCH
                        dve.wait_ge(s_ready, k + 1)
                        chain.link(nc.vector.reduce_max(chunk_max[:, par, j:j + 1],
                                                        score_banks[:, 2 * (u % 2):2 * (u % 2) + 2, :]
                                                        .rearrange("p a n -> p (a n)"), AX_X))
                        nc.vector.tensor_scalar(exp_bias[:, u:u + 1], chunk_max[:, par, j:j + 1], neg_down[:, 0:1],
                                                LOG_UP, ALU.mult, ALU.add).then_inc(bias_ready, 1)
                        if j == NCH - 1:
                            chain.link(nc.vector.reduce_max(row_max1[:, par:par + 1], chunk_max[:, par, :], AX_X))
                            nc.vector.tensor_scalar(below_max[:, par, :], chunk_max[:, par, :],
                                                    row_max1[:, par:par + 1], down[:, 0:1], ALU.subtract, ALU.mult
                                                    ).then_inc(below_ready, 1)
                        if not (first and par == 0):
                            if j == 0:
                                weigh_chunks(t * 2 + par - 1, 1 - par)
                            elif j == 1:
                                weigh_values(t * 2 + par - 1, 1 - par)
                            elif j == 2:
                                split_values(1 - par)

                main = start + L0 + BETWEEN
                rebase(main)
                steps1(0, True)
                with dve.Fori(1, T // 2) as t:
                    rebase(main + t * (2 * LINK_BLOCK) - LINK_W)
                    steps1(t, False)
                    assert chain.n == 2 * LINK_BLOCK
                rebase(start + PER_IMAGE - LINK_W)
                weigh_chunks(T - 1, 1)
                weigh_values(T - 1, 1)
                split_values(1)
                dve.wait_ge(pv1_done, (image + 1) * NCH * T + FREE_E1)
                for j in range(NCH):
                    blocks = slice(j * BPC, (j + 1) * BPC)
                    nc.vector.scalar_tensor_tensor(
                        out=x_mid[:, blocks, :].rearrange("p k c -> p (k c)"), in0=sum_banks[:, j, :],
                        scalar=gam_down1[:, :], in1=x_mid[:, blocks, :].rearrange("p k c -> p (k c)"),
                        op0=ALU.mult, op1=ALU.add).then_inc(y_ready, 1)


_INS = ['x', 'L0_conv_wf', 'L0_conv_bf', 'L0_conv_wg', 'L0_conv_bg', 'L0_conv_wh', 'L0_conv_bh', 'L0_conv_gamma',
        'L1_conv_Wq', 'L1_conv_bq', 'L1_conv_Wk', 'L1_conv_bk', 'L1_conv_Wv', 'L1_conv_bv', 'L1_conv_gamma']


def kernel(**inputs):
    import numpy as _np
    import concourse.bacc as _bacc
    from concourse import mybir as _mybir
    from concourse.bass_utils import run_bass_kernel_spmd as _run

    nc = _bacc.Bacc("TRN2", target_bir_lowering=False, num_devices=1)
    arrays, args = {}, []
    for name in _INS:
        a = _np.ascontiguousarray(inputs[name])
        arrays[f"in_{name}_dram"] = a
        args.append(nc.dram_tensor(f"in_{name}_dram", a.shape, _mybir.dt.from_np(a.dtype), kind="ExternalInput").ap())
    shape = tuple(inputs['x'].shape)
    args.append(nc.dram_tensor("out_0_dram", shape, _mybir.dt.float32, kind="ExternalOutput").ap())
    attention_pair_kernel(nc, *args)
    r = _run(nc, [arrays], core_ids=[0])
    return r.results[0]["out_0_dram"]
```

```python
import math
from contextlib import ExitStack

import concourse.bass as bass
from concourse import mybir

F32 = mybir.dt.float32
F16 = mybir.dt.float16
BF16 = mybir.dt.bfloat16
I32 = mybir.dt.int32
ALU = mybir.AluOpType
ACT = mybir.ActivationFunctionType
AX_X = mybir.AxisListType.X
ds = bass.ds

P = 128
BANK = 512
EXPONENT_BITS = 0x7F800000
EXP_UP = 15
LOG_UP = EXP_UP * math.log(2.0)
HALF_TOP = 14


def attention_pair_kernel(nc, x, wf, bf, wg, bg, wh, bh, gamma0, wq, bq, wk, bk, wv, bv, gamma1, out):
    B, H, W, C = x.shape
    N = H * W
    CK = wf.shape[1]
    T = N // P
    C1 = C + 1
    NQ = N // BANK
    CH = 2 * BANK
    NCH = N // CH
    BPC = CH // P
    KS = 9 * CK
    KM = KS + 3
    MROW = 64
    GFW = 2 * CK
    PW = GFW + C
    VW = C + 1
    TR = BANK // P
    RND = T // TR
    RT = T // BPC
    ATN = N // BANK
    ATS = T * ATN
    U0 = 8
    U1 = 2 * NCH
    RING = 4
    LAG0 = 5
    LAG1 = 7
    STEPS0, STEPS1 = NCH * T, T * NCH
    TURN = 8
    HIGH = [{"act": [0, 1, 2, 4, 5, 6, 7], "pool": [3]}, {"act": [0, 2, 4, 6], "pool": [1, 5]}]
    LOW = [{"dve": [0, 2, 4], "pool": [1, 3, 5, 6, 7]}, {"pool": [0, 1, 2, 4, 5, 6]}]
    WHOLE = 3
    DVE_BEHIND = 1
    FREE_ST, FREE_A, FREE_E0, FREE_S1, FREE_E1 = 2, 4, U0, 2, U1
    FREE_LOW = RING
    FREE = 1
    EARLY = U0 // 4
    MROW_AFTER = 2
    TILES = BPC * ATN
    LINED_UP = T // U0 - 1
    assert BPC == EARLY * (LINED_UP + 1)
    assert U0 == U1 == TURN and N % (P * BPC) == 0 and C == 64 and CK == 8 and NCH == 4

    x_t = x.rearrange("b h w c -> b (h w) c").rearrange("b (p t) c -> b p t c", p=P)
    out_t = out.rearrange("b h w c -> b (h w) c").rearrange("b (p t) c -> b p t c", p=P)

    with ExitStack() as ctx:
        def sb(name, shape, dt):
            return ctx.enter_context(nc.sbuf_tensor(name, shape, dt))

        def sem(name):
            return ctx.enter_context(nc.semaphore(name))

        score_banks = ctx.enter_context(nc.psum_tensor("score_banks", [P, 4, BANK], F32))
        sum_banks = ctx.enter_context(nc.psum_tensor("sum_banks", [P, 4, BANK], F32))

        x_in = sb("x_in", [P, T + BPC, C], F32)
        x_mid = sb("x_mid", [P, T, C], F32)
        x_tr = sb("x_tr", [C1, N], F32)
        w0 = sb("w0", [C1, PW], F32)
        w1 = sb("w1", [C1, 2, C], F32)
        w1s = sb("w1s", [C1, 2 * C], F32)
        w1v = sb("w1v", [C1, C], F32)
        w_row = sb("w_row", [C1, 1], F32)
        x_abs = sb("x_abs", [C1, 1], F32)
        bound_in = sb("bound_in", [C1, 1], F32)
        gammas = sb("gammas", [P, 2], F32)
        ident = sb("ident", [P, P], F32)
        ident_b = sb("ident_b", [P, P], BF16)
        ones = sb("ones", [C1, 1], F32)
        zeros = sb("zeros", [P, P], F16)
        ones_b = sb("ones_b", [P, 1], BF16)
        credit = sb("credit", [P, 13], F32)
        proj = sb("proj", [P, T, PW + 1], F32)
        piece = [sb(f"piece{k}", [P, T, GFW], BF16) for k in range(3)]
        g_stack = sb("g_stack", [P, 2, T, KM + 1], BF16)
        f_stack = sb("f_stack", [P, T, KM + 1], BF16)
        g_tr = sb("g_tr", [KM, 2, N], BF16)
        f_tr = sb("f_tr", [KM, 2, N], BF16)
        tile_max = sb("tile_max", [P, BPC, ATN], F32)
        row_max0 = sb("row_max0", [P, BPC], F32)
        max_rest = sb("max_rest", [P, BPC], F32)
        inv_sum0 = sb("inv_sum0", [P, 2, BPC // 2], F32)
        inv_gam0 = sb("inv_gam0", [P, 2, BPC // 2], F32)
        att0 = sb("att0", [P, BPC, C], F32)
        probs = sb("probs", [P, RING, CH], F32)
        e_high = sb("e_high", [P, U1, CH], F16)
        e_whole = sb("e_whole", [P, U1 // 4, CH], F32)
        e_low = sb("e_low", [P, U1, CH], F16)
        h_high = sb("h_high", [P, 2, T, VW], F16)
        h_low = sb("h_low", [P, 2, T, C], F16)
        v_abs = sb("v_abs", [P, 2], F32)
        v_top = sb("v_top", [P, 2], F32)
        v_top1 = sb("v_top1", [P, 2], F32)
        v_pow2 = sb("v_pow2", [P, 2], F32)
        v_inv = sb("v_inv", [P, 2], F32)
        v_up = sb("v_up", [P, 2], F32)
        gam_down0 = sb("gam_down0", [P, 2], F32)
        gam_down1 = sb("gam_down1", [P, 1], F32)
        q_split = sb("q_split", [P, N], F16)
        k_high = sb("k_high", [P, N], F16)
        k_low = sb("k_low", [P, N], F16)
        v1 = sb("v1", [P, T, C], F32)
        v_scaled = sb("v_scaled", [P, 2, NCH, C], F32)
        v_high = sb("v_high", [P, 2, NCH, C], F16)
        v_low = sb("v_low", [P, 2, NCH, C], F16)
        log_up = sb("log_up", [P, 1], F32)
        bound = sb("bound", [P, 1], F32)
        pow2 = sb("pow2", [P, 1], F32)
        inv_pow2 = sb("inv_pow2", [P, 1], F32)
        up = sb("up", [P, 1], F32)
        down1 = sb("down1", [P, 1], F32)
        down = sb("down", [P, 1], F32)
        neg_down = sb("neg_down", [P, 1], F32)
        chunk_max = sb("chunk_max", [P, 2, NCH], F32)
        exp_bias = sb("exp_bias", [P, U1], F32)
        row_max1 = sb("row_max1", [P, 2], F32)
        below_max = sb("below_max", [P, 2, NCH], F32)
        chunk_w = sb("chunk_w", [P, 2, NCH], F32)
        part_sum = sb("part_sum", [P, 2, NCH], F32)
        part_scr = sb("part_scr", [P, NCH], F32)
        row_sum1 = sb("row_sum1", [P, 2], F32)
        inv_sum1 = sb("inv_sum1", [P, 2], F32)
        norm_w = sb("norm_w", [P, 2, NCH], F32)

        w_in, x_loaded, y_stored = sem("w_in"), sem("x_loaded"), sem("y_stored")
        ident_zero, ident_f, ident_ready, const_ready = sem("ident_zero"), sem("ident_f"), sem("ident_ready"), sem("const_ready")
        w_ready = sem("w_ready")
        xt_ps, xt_act, xt_dve = ([sem(f"{n}_{layer}") for layer in range(2)] for n in ("xt_ps", "xt_act", "xt_dve"))
        pj_ps, pj_act, pj_dve = sem("pj_ps"), sem("pj_act"), sem("pj_dve")
        piece_ready, g_stacked, f_stacked = sem("piece_ready"), sem("g_stacked"), sem("f_stacked")
        ft_ps, gt_ps, ft_sb, gt_sb = sem("ft_ps"), sem("gt_ps"), sem("ft_sb"), sem("gt_sb")
        a_ready, a_used = sem("a_ready"), sem("a_used")
        max_split, mrow_ps, mrow_sb = sem("max_split"), sem("mrow_ps"), sem("mrow_sb")
        st_ready, exp0_done, pv0_done = sem("st_ready"), sem("exp0_done"), sem("pv0_done")
        att0_ready, x_mid_ready = sem("att0_ready"), sem("x_mid_ready")
        bound_sent, bound_ps, w1s_ready = sem("bound_sent"), sem("bound_ps"), sem("w1s_ready")
        v1_ps, v1_sb = sem("v1_ps"), sem("v1_sb")
        qk_ps, high_done, low_done = sem("qk_ps"), sem("high_done"), sem("low_done")
        k_copied = [sem(f"k_copied_{j}") for j in range(NCH)]
        s_ready, bias_ready, exp1_done, pv1_done = sem("s_ready"), sem("bias_ready"), sem("exp1_done"), sem("pv1_done")
        below_ready, chunk_w_ready, y_ready = sem("below_ready"), sem("chunk_w_ready"), sem("y_ready")
        dve_step = sem("dve_step")
        high_by = {"act": sem("high_by_act"), "pool": sem("high_by_pool")}
        low_by = {"dve": sem("low_by_dve"), "pool": sem("low_by_pool")}
        v_abs_ready, v_top_ready = ([sem(f"{n}_{layer}") for layer in range(2)] for n in ("v_abs_ready", "v_top_ready"))
        h_scale_ready = sem("h_scale_ready")
        h_scaled_ready, h_high_ready, h_low_ready = sem("h_scaled_ready"), sem("h_high_ready"), sem("h_low_ready")
        v_split_ready = sem("v_split_ready")
        pool_go = sem("pool_go")

        block = ctx.enter_context(nc.Block())
        N_W = 14

        def wait_x_tr(eng, image, layer, r=RT - 1):
            eng.wait_ge(xt_act[layer], image * RT + r + 1)
            eng.wait_ge(xt_dve[layer], image * RT + r + 1)

        def loads(image, early=False):
            return image + 1 if early else image * 2

        g_cols = g_tr[:, :, :].rearrange("k a n -> k (a n)")
        g_blocks = g_stack[:, :, :, :].rearrange("p a t c -> p (a t) c")

        def place(chunk):
            return chunk % (2 * NCH)

        def half_of_blocks(r, odd):
            return x_tr[0:C, r * CH:(r + 1) * CH].rearrange("c (k a n) -> c k a n", a=2, n=P)[:, :, odd, :]

        def part_done(table, sems, layer, image, t, u):
            t, u = t + u // TURN, u % TURN
            by = next(e for e, slots in table[layer].items() if u in slots)
            n = [len(table[l].get(by, [])) for l in range(2)]
            before = n[0] * STEPS0 // TURN if layer == 1 else 0
            rank = table[layer][by].index(u) + 1
            return sems[by], image * ((n[0] * STEPS0 + n[1] * STEPS1) // TURN) + before + t * n[layer] + rank

        def wait_high(eng, layer, image, t, u):
            eng.wait_ge(*part_done(HIGH, high_by, layer, image, t, u))

        def wait_low(eng, layer, image, t, u):
            done, count = part_done(LOW, low_by, layer, image, t, u)
            eng.wait_ge(done, count + FREE_LOW)

        def split_high(copy, slot, u):
            return copy(e_high[:, slot, :], probs[:, u % RING, :])

        def split_low(subtract, slot, u):
            return subtract(e_low[:, slot, :], probs[:, u % RING, :], e_high[:, slot, :], ALU.subtract)

        @block.sync
        def _(sp):
            def load(image, first_block):
                sp.dma_start(x_in[:, first_block:first_block + T, :], x_t[image]).then_inc(x_loaded, 16)

            for col, w_, b_ in ((0, wg, bg), (CK, wf, bf), (GFW, wh, bh)):
                n = w_.shape[1]
                sp.dma_start(w0[0:C, col:col + n], w_).then_inc(w_in, 16)
                sp.dma_start(w0[C:C1, col:col + n], b_.unsqueeze(0)).then_inc(w_in, 16)
            load(0, 0)
            for k, w_, b_ in ((0, wq, bq), (1, wk, bk)):
                sp.dma_start(w1[0:C, k, :], w_).then_inc(w_in, 16)
                sp.dma_start(w1[C:C1, k, :], b_.unsqueeze(0)).then_inc(w_in, 16)
            sp.dma_start(w1v[0:C, :], wv).then_inc(w_in, 16)
            sp.dma_start(w1v[C:C1, :], bv.unsqueeze(0)).then_inc(w_in, 16)
            sp.dma_start(gammas[:, 0:1], gamma0.partition_broadcast(P)).then_inc(w_in, 16)
            sp.dma_start(gammas[:, 1:2], gamma1.partition_broadcast(P)).then_inc(w_in, 16)

            sp.wait_ge(xt_ps[0], RT)
            load(1 % B, 0)
            sp.wait_ge(xt_ps[0], 2 * RT)
            load(0, BPC)
            with sp.Fori(0, B) as image:
                ahead, following = (image + 2) % B, (image + 1) % B
                sp.wait_ge(x_mid_ready, image * NCH + NCH - 1 + FREE)
                load(ahead, 0)
                sp.wait_ge(xt_ps[1], (image + 1) * RT)
                load(following, BPC)
                for j in range(NCH):
                    cols = slice(j * CH, (j + 1) * CH)
                    for part, done in ((k_high, high_done), (k_low, low_done)):
                        sp.wait_ge(done, 2 * (image * NQ + (j + 1) * (CH // BANK)))
                        sp.dma_start(part[0:C, cols], part[C:P, cols]).then_inc(k_copied[j], 16)
                for j in range(NCH):
                    sp.wait_ge(y_ready, image * NCH + j + 1 + FREE)
                    sp.dma_start(out_t[image, :, j * BPC:(j + 1) * BPC, :],
                                 x_mid[:, j * BPC:(j + 1) * BPC, :]).then_inc(y_stored, 16)
            sp.wait_ge(x_loaded, (3 + 2 * B) * 16)
            sp.wait_ge(y_stored, 16 * (NCH * B + FREE))

        @block.gpsimd
        def _(pool):
            nc.gpsimd.memset(ident[:], 0.0).then_inc(ident_zero, 1)
            pool.wait_ge(ident_zero, 1)
            nc.gpsimd.affine_select(out=ident[:], in_=ident[:], compare_op=ALU.not_equal, fill=1.0, base=0,
                                    pattern=[[-1, P]], channel_multiplier=1).then_inc(ident_f, 1)
            pool.wait_ge(ident_f, 1)
            nc.gpsimd.tensor_copy(ident_b[:], ident[:]).then_inc(ident_ready, 1)
            nc.gpsimd.memset(g_stack[:], 0.0).then_inc(const_ready, 1)
            nc.gpsimd.memset(f_stack[:], 1.0).then_inc(const_ready, 1)
            nc.gpsimd.memset(proj[:, :, PW:PW + 1], 1.0).then_inc(const_ready, 1)
            nc.gpsimd.memset(ones[:], 1.0).then_inc(const_ready, 1)
            nc.gpsimd.memset(ones_b[:], 1.0).then_inc(const_ready, 1)
            nc.gpsimd.memset(credit[:, 0:1], 0.0).then_inc(exp0_done, FREE_ST)
            nc.gpsimd.memset(credit[:, 1:2], 0.0).then_inc(a_used, FREE_A)
            nc.gpsimd.memset(credit[:, 2:3], 0.0).then_inc(pv0_done, FREE_E0)
            nc.gpsimd.memset(credit[:, 3:4], 0.0).then_inc(exp1_done, FREE_S1)
            nc.gpsimd.memset(credit[:, 4:5], 0.0).then_inc(pv1_done, FREE_E1)
            nc.gpsimd.memset(credit[:, 5:6], 0.0).then_inc(low_by["pool"], FREE_LOW)
            nc.gpsimd.memset(credit[:, 6:7], 0.0).then_inc(low_by["dve"], FREE_LOW)
            nc.gpsimd.memset(log_up[:], LOG_UP).then_inc(const_ready, 1)
            for n, (free, by) in enumerate(((y_ready, FREE), (att0_ready, FREE), (x_mid_ready, FREE), (y_stored, 16 * FREE),
                                               (h_low_ready, FREE))):
                nc.gpsimd.memset(credit[:, 8 + n:9 + n], 0.0).then_inc(free, by)
            nc.gpsimd.memset(zeros[:], 0.0).then_inc(const_ready, 1)
            nc.gpsimd.memset(h_high[:, :, :, C:VW], 1.0).then_inc(const_ready, 1)
            pool.wait_ge(const_ready, 10)

            def largest_value(image, layer):
                pool.wait_ge(v_abs_ready[layer], image + 1)
                pool.sem_inc(pool_go, 1)
                nc.gpsimd.partition_all_reduce(v_top[:, layer:layer + 1], v_abs[:, layer:layer + 1], P,
                                               bass.bass_isa.ReduceOp.max).then_inc(v_top_ready[layer], 1)

            def split(layer, image, t, u):
                high, low = u in HIGH[layer]["pool"], u in LOW[layer]["pool"]
                k = t * TURN + u
                step = image * STEPS0 + k
                if high:
                    pool.wait_ge(*((exp0_done, step + 1 + FREE_ST) if layer == 0 else (exp1_done, step + 1 + FREE_S1)))
                    pool.wait_ge(pv0_done if layer == 0 else pv1_done, step + 1)
                    pool.sem_inc(pool_go, 1)
                    split_high(lambda o, i: nc.gpsimd.tensor_scalar(o, i, 1.0, 0.0, ALU.mult, ALU.add), u, u
                               ).then_inc(high_by["pool"], 1)
                if low:
                    wait_high(pool, layer, image, t, u)
                    split_low(nc.gpsimd.tensor_tensor, u, u).then_inc(low_by["pool"], 1)

            def steps1(image, t):
                for u in range(U1):
                    split(1, image, t, u)

            def stack_g(image, par):
                for k in range(3):
                    pool.wait_ge(piece_ready, image * 3 + k + 1)
                    dst = g_stack[:, par, :, 3 * CK * k:3 * CK * (k + 1)].rearrange("p t (r c) -> p t r c", r=3)
                    src = piece[k][:, :, 0:CK].unsqueeze(2).to_broadcast([P, T, 3, CK])
                    one = ones_b[:, :].unsqueeze(2).unsqueeze(3).to_broadcast([P, T, 3, CK])
                    nc.gpsimd.tensor_tensor(dst, src, one, ALU.mult).then_inc(g_stacked, 1)

            def low_values(image, par, r):
                blocks = slice(r * BPC, (r + 1) * BPC)
                pool.wait_ge(h_high_ready, image * NCH + r + 1)
                nc.gpsimd.tensor_tensor(h_low[:, par, blocks, :], proj[:, blocks, GFW:PW],
                                        h_high[:, par, blocks, 0:C], ALU.subtract).then_inc(h_low_ready, 1)

            with pool.Fori(0, 2) as image:
                stack_g(image, image % 2)
                largest_value(image, 0)
                for r in range(NCH):
                    low_values(image, image % 2, r)
            with pool.Fori(0, B) as image:
                def steps0(q, t):
                    for u in range(U0):
                        split(0, image, q * (T // U0) + t, u)

                def residual(q):
                    pool.wait_ge(x_loaded, 16 * (2 * image + 3))
                    pool.wait_ge(y_stored, (image * NCH + FREE) * 16)
                    pool.wait_ge(att0_ready, image * NCH + q + 1 + FREE)
                    nc.gpsimd.tensor_tensor(x_mid[:, ds(q * BPC, BPC), :], att0[:, :, :],
                                            x_in[:, ds(q * BPC + BPC, BPC), :], ALU.add).then_inc(x_mid_ready, 1)

                steps0(0, 0)
                with pool.Fori(0, NCH - 1) as q:
                    with pool.Fori(1, T // U0) as t:
                        steps0(q, t)
                    steps0(q + 1, 0)
                    residual(q)
                with pool.Fori(1, T // U0) as t:
                    steps0(NCH - 1, t)
                residual(NCH - 1)
                par = image % 2
                stack_g(image + 2, par)
                largest_value(image + 2, 0)
                largest_value(image, 1)
                for r in range(NCH):
                    low_values(image + 2, par, r)
                with pool.Fori(0, T // 2) as t:
                    steps1(image, t)

        @block.tensor
        def _(pe):
            def transposes(image, layer, src):
                for r in range(RT):
                    if layer == 1:
                        pe.wait_ge(x_mid_ready, image * NCH + r + 1 + FREE)
                        pe.wait_ge(pj_act if r % 2 == 0 else pj_dve, (image + 2) * (RND // 2) + (RND - 4 + r) // 2 + 1)
                    for k in range(BPC // 2):
                        t = r * BPC + 2 * k
                        mm = nc.tensor.transpose(score_banks[:, r, k * P:(k + 1) * P],
                                                 src[:, t:t + 2, :].rearrange("p a c -> p (a c)"), ident[:, :])
                    mm.then_inc(xt_ps[layer], 1)

            def project0(image, early):
                pe.wait_ge(x_loaded, 16 * loads(image, early))
                transposes(image, 0, x_in)
                pe.wait_ge(h_low_ready, image * NCH + FREE)
                for r in range(RND):
                    if r < RT:
                        wait_x_tr(pe, image, 0, r)
                    if r >= 4:
                        pe.wait_ge(pj_act if r % 2 == 0 else pj_dve, image * (RND // 2) + (r - 4) // 2 + 1)
                    for k in range(TR):
                        t = r * TR + k
                        mm = nc.tensor.matmul(score_banks[:, r % 4, k * P:k * P + PW], x_tr[:, t * P:(t + 1) * P],
                                              w0[:, :], start=True, stop=True)
                    mm.then_inc(pj_ps, 1)

            def transpose_stacks(image, par, rounds=range(NCH)):
                for r in rounds:
                    for src, stacked, used, ready, which in ((f_stack, f_stacked, ft_sb, ft_ps, 0),
                                                             (g_stack, g_stacked, gt_sb, gt_ps, 1)):
                        if r == 0:
                            pe.wait_ge(stacked, (image + 1) * 3)
                        if r >= 2:
                            pe.wait_ge(used, image * NCH + r - 1)
                        bank = sum_banks[0:KM, 2 * (r % 2) + which, :].bitcast(BF16)
                        rows = KM if which == 0 else KS
                        for k in range(BPC):
                            t = r * BPC + k
                            blk = src[:, t, 0:rows] if which == 0 else src[:, par, t, 0:rows]
                            mm = nc.tensor.transpose(bank[0:rows, k * P:(k + 1) * P], blk, ident_b[:, :])
                        mm.then_inc(ready, 1)

            def max_pass_tiles(ahead, blk, js, banks=2):
                image, par, q = ahead
                for j in js:
                    pe.wait_ge(a_used, image * ATS + q * TILES + blk * ATN + j + 1 + FREE_A - banks)
                    nc.tensor.matmul(sum_banks[:, (2 + j % banks) % 4, :], g_tr[0:KS, par, ds(q * CH + blk * P, P)],
                                     f_tr[0:KS, par, j * BANK:(j + 1) * BANK], start=True, stop=True).then_inc(a_ready, 1)

            def max_rows(ahead, tiles_ahead):
                image, par, q = ahead
                pe.wait_ge(a_used, image * ATS + (q + 1) * TILES + tiles_ahead + FREE_A)
                pe.wait_ge(max_split, image * NCH + q + 1)
                for k in range(BPC):
                    mm = nc.tensor.matmul(sum_banks[0:KM, 2 + k // 4, (k % 4) * P:(k % 4 + 1) * P],
                                          g_stack[:, par, q * BPC + k, 0:KM], ident_b[:, :], start=True, stop=True)
                mm.then_inc(mrow_ps, 1)

            def scores0(image, par, q, i, u):
                step = image * NCH * T + q * T + i
                pe.wait_ge(exp0_done, step + 1)
                for h in range(2):
                    mm = nc.tensor.matmul(score_banks[:, 2 * (u % 2) + h, :], f_tr[0:KM, par, ds(i * P, P)],
                                          g_tr[0:KM, par, ds(q * CH + h * BANK, BANK)], start=True, stop=True)
                mm.then_inc(st_ready, 1)

            def products(low_slot, bank_of, width, pitch, highs, lows):
                for n in range(BPC):
                    bank, o = bank_of(n)
                    for e in (e_high, e_low):
                        for v in (highs, lows):
                            mm = nc.tensor.matmul(sum_banks[:, bank, o:o + v.shape[-1]], e[:, low_slot, n * P:(n + 1) * P],
                                                  v, start=False, stop=True, skip_group_check=True)
                return mm

            def open_sums(banks):
                for j in range(banks):
                    nc.tensor.matmul(sum_banks[:, j, :], zeros[:, :],
                                     zeros[:, :].unsqueeze(1).to_broadcast([P, BANK // P, P]), start=True, stop=True,
                                     skip_group_check=True)

            def values0(image, par, q, t, u):
                t, u = t + u // U0, u % U0
                i = t * U0 + u
                wait_low(pe, 0, image, q * (T // U0) + t, u)
                products(u, lambda n: (n // 4, (n % 4) * VW), VW, VW,
                         h_high[:, par, i, :], h_low[:, par, i, :]).then_inc(pv0_done, 1)

            def pair(u):
                return range(2 * (u % 4), 2 * (u % 4) + 2)

            def first_steps0(image, par, q, behind, ahead):
                with pe.Fori(0, 1) as t:
                    first_turn0(image, par, q, behind, ahead, t)

            def first_turn0(image, par, q, behind, ahead, t):
                if behind is None:
                    pe.wait_ge(exp1_done, image * STEPS1 + FREE_S1)
                pe.wait_ge(mrow_sb, image * NCH + q + 1)
                for u in range(U0):
                    scores0(image, par, q, t * U0 + u, u)
                    if behind is None and u == 0:
                        pe.wait_ge(y_ready, image * NCH + FREE)
                    max_pass_tiles(ahead, EARLY + t * EARLY + u // 4, pair(u))
                    if behind is not None and u < LAG0:
                        values0(image, par, behind, t + T // U0, u - LAG0)
                    if u == LAG0 + 1:
                        pe.wait_ge(att0_ready, image * NCH + q + FREE)
                        pe.wait_ge(h_low_ready, (image + 1) * NCH + FREE)
                        open_sums(2)
                        values0(image, par, q, t, 0)
                    if u > LAG0:
                        values0(image, par, q, t, u - LAG0)

            def other_steps0(image, par, q, ahead, ahead2):
                def steps(t, last):
                    for u in range(U0):
                        late = last and u == MROW_AFTER + 1
                        tiles = (ahead2, u // 4, pair(u)) if last else (ahead, EARLY + t * EARLY + u // 4, pair(u))
                        scores0(image, par, q, t * U0 + u, u)
                        if not late:
                            max_pass_tiles(*tiles)
                        values0(image, par, q, t, u - LAG0)
                        if last and u == MROW_AFTER:
                            max_rows(ahead, 2 * (MROW_AFTER + 1))
                        if late:
                            pe.wait_ge(mrow_sb, image * NCH + q + 2)
                            max_pass_tiles(*tiles)

                with pe.Fori(1, LINED_UP) as t:
                    steps(t, False)
                with pe.Fori(LINED_UP, LINED_UP + 1) as t:
                    steps(t, True)

            def scores1(image, i, k, u):
                pe.wait_ge(exp1_done, image * STEPS1 + k + 1)
                for h in range(2):
                    col = (u % NCH) * CH + h * BANK
                    bank = score_banks[:, 2 * (u % 2) + h, :]
                    nc.tensor.matmul(bank, q_split[:, ds(i * P, P)], k_high[:, col:col + BANK], start=True, stop=False)
                    mm = nc.tensor.matmul(bank, q_split[:, ds(i * P, P)], k_low[:, col:col + BANK],
                                          start=False, stop=True)
                mm.then_inc(s_ready, 1)

            def values1(image, t, u):
                t, u = t + u // U1, u % U1
                i, j = t * 2 + u // NCH, u % NCH
                if j == 0:
                    pe.wait_ge(v_split_ready, image * T + i + 1)
                if j == WHOLE:
                    pe.wait_ge(exp1_done, image * STEPS1 + t * U1 + u + 1 + FREE_S1)
                    for n in range(BPC):
                        mm = nc.tensor.matmul(sum_banks[:, j, n * C:(n + 1) * C], e_whole[:, u // 4, n * P:(n + 1) * P],
                                              v_scaled[:, u // NCH, j, :], start=False, stop=True,
                                              skip_group_check=True)
                    mm.then_inc(pv1_done, 1)
                    return
                wait_low(pe, 1, image, t, u)
                products(u, lambda n: (j, n * C), C, C, v_high[:, u // NCH, j, :],
                         v_low[:, u // NCH, j, :]).then_inc(pv1_done, 1)

            pe.wait_ge(ident_ready, 1)
            pe.wait_ge(const_ready, 10)
            pe.wait_ge(w_in, 16 * N_W)
            with pe.Fori(0, 2) as image:
                project0(image, True)
                pe.wait_ge(pj_act, (image + 1) * (RND // 2))
                pe.wait_ge(pj_dve, (image + 1) * (RND // 2))
                transpose_stacks(image, image % 2)
                pe.wait_ge(ft_sb, (image + 1) * NCH)
                pe.wait_ge(gt_sb, (image + 1) * NCH)
            for chunk, blocks in ((0, BPC), (1, EARLY)):
                with pe.Fori(0, blocks) as blk:
                    max_pass_tiles((0, 0, chunk), blk, range(ATN), 4)
            max_rows((0, 0, 0), EARLY * ATN)
            with pe.Fori(0, B) as image:
                par, next_par = image % 2, (image + 1) % 2
                first_steps0(image, par, 0, None, (image, par, 1))
                with pe.Fori(0, NCH - 2) as q:
                    other_steps0(image, par, q, (image, par, q + 1), (image, par, q + 2))
                    first_steps0(image, par, q + 1, q, (image, par, q + 2))
                other_steps0(image, par, NCH - 2, (image, par, NCH - 1), (image + 1, next_par, 0))
                first_steps0(image, par, NCH - 1, NCH - 2, (image + 1, next_par, 0))
                other_steps0(image, par, NCH - 1, (image + 1, next_par, 0), (image + 1, next_par, 1))
                for u in range(U0 - LAG0, U0):
                    values0(image, par, NCH - 1, LINED_UP, u)
                pe.wait_ge(exp0_done, (image + 1) * NCH * T + FREE_ST)
                project0(image + 2, False)
                transposes(image, 1, x_mid)
                for r in range(NCH):
                    wait_x_tr(pe, image, 1, r)
                    for k in range(BPC):
                        t = r * BPC + k
                        mm = nc.tensor.matmul(score_banks[:, r, k * C:(k + 1) * C], x_tr[:, t * P:(t + 1) * P],
                                              w1v[:, :], start=True, stop=True)
                    mm.then_inc(v1_ps, 1)
                    if r == NCH - 2:
                        pe.wait_ge(bound_sent, image + 1)
                        nc.tensor.matmul(sum_banks[:, 0, 0:1], bound_in[:, :].to_broadcast([C1, P]), ones[:, :],
                                         start=True, stop=True).then_inc(bound_ps, 1)
                pe.wait_ge(w1s_ready, image + 1)
                pe.wait_ge(mrow_sb, (image + 1) * NCH + 1)
                pe.wait_ge(att0_ready, (image + 1) * NCH + FREE)
                pe.wait_ge(a_used, ((image + 1) * NCH + 1) * TILES + EARLY * ATN + FREE_A)
                for c in range(NQ):
                    if c < 4:
                        pe.wait_ge(v1_sb, image * NCH + c + 1)
                    else:
                        pe.wait_ge(low_done, 2 * (image * NQ + c - 3))
                    nc.tensor.matmul(score_banks[:, c % 4, :], w1s[:, :], x_tr[:, c * BANK:(c + 1) * BANK],
                                     start=True, stop=True).then_inc(qk_ps, 1)


                def steps1(t, first):
                    for u in range(U1):
                        if first and u < 2:
                            pe.wait_ge(low_done, 2 * ((image + 1) * NQ - 2 + 2 * u))
                        if first and u < NCH:
                            pe.wait_ge(k_copied[u], 32 * (image + 1))
                        scores1(image, t * 2 + u // NCH, t * U1 + u, u)
                        if first and 0 < u <= NCH:
                            transpose_stacks(image + 2, par, [u - 1])
                        if first and u == LAG1:
                            pe.wait_ge(ft_sb, (image + 3) * NCH)
                            pe.wait_ge(gt_sb, (image + 3) * NCH)
                            open_sums(NCH)
                        if not first or u >= LAG1:
                            values1(image, t, u - LAG1)

                steps1(0, True)
                with pe.Fori(1, T // 2) as t:
                    steps1(t, False)
                for u in range(U1 - LAG1, U1):
                    values1(image, T // 2 - 1, u)

        @block.scalar
        def _(act):
            def transposed(image, layer):
                for r in range(RT):
                    act.wait_ge(xt_ps[layer], image * RT + r + 1)
                    nc.scalar.copy(half_of_blocks(r, 0), score_banks[0:C, r, :].rearrange("c (k n) -> c k n", n=P)
                                   ).then_inc(xt_act[layer], 1)

            def max_rows(chunk):
                act.wait_ge(mrow_ps, chunk + 1)
                nc.scalar.copy(g_cols[MROW:KM, ds(place(chunk) * CH, CH)].rearrange("p (a n) -> p a n", a=2),
                               sum_banks[MROW:KM, 2:4, :]).then_inc(mrow_sb, 1)

            def chunk0(image, q):
                def steps(t, last):
                    for u in range(U0):
                        step = image * NCH * T + q * T + t * U0 + u
                        act.wait_ge(st_ready, step + 1)
                        wait_low(act, 0, image, q * (T // U0) + t, u - RING)
                        nc.scalar.activation(probs[:, u % RING, :].rearrange("p (a n) -> p a n", a=2),
                                             score_banks[:, 2 * (u % 2):2 * (u % 2) + 2, :],
                                             ACT.Exp, bias=log_up[:, 0:1]).then_inc(exp0_done, 1)
                        if u in HIGH[0]["act"]:
                            act.wait_ge(exp0_done, step + 1 + FREE_ST)
                            act.wait_ge(pv0_done, step + 1)
                            split_high(nc.scalar.copy, u, u).then_inc(high_by["act"], 1)
                        if last and u == MROW_AFTER:
                            max_rows(image * NCH + q + 1)

                with act.Fori(0, LINED_UP) as t:
                    steps(t, False)
                steps(LINED_UP, True)

            def project0(image):
                transposed(image, 0)
                for r in range(0, RND, 2):
                    act.wait_ge(pj_ps, image * RND + r + 1)
                    nc.scalar.copy(proj[:, r * TR:(r + 1) * TR, 0:PW],
                                   score_banks[:, r % 4, :].rearrange("p (k n) -> p k n", k=TR)[:, :, 0:PW]
                                   ).then_inc(pj_act, 1)

            def stack_f(image):
                for k in range(3):
                    act.wait_ge(piece_ready, image * 3 + k + 1)
                    dst = f_stack[:, :, 0:KS].rearrange("p t (r k c) -> p t r k c", r=3, k=3)[:, :, :, k, :]
                    src = piece[k][:, :, CK:GFW].unsqueeze(2).to_broadcast([P, T, 3, CK])
                    nc.scalar.copy(dst, src).then_inc(f_stacked, 1)

            def transposed_f(image, par, rounds=range(NCH)):
                for r in rounds:
                    act.wait_ge(ft_ps, image * NCH + r + 1)
                    nc.scalar.copy(f_tr[0:KM, par, r * CH:(r + 1) * CH],
                                   sum_banks[0:KM, 2 * (r % 2), :].bitcast(BF16)).then_inc(ft_sb, 1)

            def scale_values(image, r):
                blocks = slice(r * BPC, (r + 1) * BPC)
                act.wait_ge(h_scale_ready, image + 1)
                nc.scalar.activation(proj[:, blocks, GFW:PW], proj[:, blocks, GFW:PW], ACT.Copy,
                                     scale=v_up[:, 0:1]).then_inc(h_scaled_ready, 1)

            def high_values(image, par, r):
                blocks = slice(r * BPC, (r + 1) * BPC)
                act.wait_ge(h_scaled_ready, image * NCH + r + 1)
                nc.scalar.copy(h_high[:, par, blocks, 0:C], proj[:, blocks, GFW:PW]).then_inc(h_high_ready, 1)

            act.wait_ge(const_ready, 10)
            with act.Fori(0, 2) as image:
                project0(image)
                stack_f(image)
                transposed_f(image, image % 2)
                for r in range(NCH):
                    scale_values(image, r)
                for r in range(NCH):
                    high_values(image, image % 2, r)
            max_rows(0)
            with act.Fori(0, B) as image:
                par = image % 2
                with act.Fori(0, NCH) as q:
                    chunk0(image, q)

                project0(image + 2)
                transposed(image, 1)
                for r in range(NCH):
                    act.wait_ge(v1_ps, image * NCH + r + 1)
                    nc.scalar.copy(v1[:, r * BPC:(r + 1) * BPC, :],
                                   score_banks[:, r, :].rearrange("p (k c) -> p k c", k=BPC)).then_inc(v1_sb, 1)
                    if r == NCH - 2:
                        stack_f(image + 2)
                for c in range(NQ):
                    act.wait_ge(qk_ps, image * NQ + c + 1)
                    for dst, rows in ((q_split, slice(0, C)), (k_high, slice(C, P))):
                        nc.scalar.copy(dst[rows, c * BANK:(c + 1) * BANK], score_banks[rows, c % 4, :]
                                       ).then_inc(high_done, 1)
                    if c % 2 == 0:
                        scale_values(image + 2, c // 2)
                    else:
                        high_values(image + 2, par, c // 2)
                def steps1(t, first):
                    for u in range(U1):
                        step = image * STEPS1 + t * U1 + u
                        act.wait_ge(bias_ready, step + 1)
                        if u % 4 == WHOLE:
                            act.wait_ge(pv1_done, step + 1)
                            dst = e_whole[:, u // 4, :]
                        else:
                            wait_low(act, 1, image, t, u - RING)
                            dst = probs[:, u % RING, :]
                        nc.scalar.activation(dst.rearrange("p (a n) -> p a n", a=2),
                                             score_banks[:, 2 * (u % 2):2 * (u % 2) + 2, :],
                                             ACT.Exp, bias=exp_bias[:, u:u + 1], scale=down[:, 0:1],
                                             accum_out=part_sum[:, u // NCH, u % NCH:u % NCH + 1]
                                             ).then_inc(exp1_done, 1)
                        if u in HIGH[1]["act"]:
                            act.wait_ge(exp1_done, step + 1 + FREE_S1)
                            act.wait_ge(pv1_done, step + 1)
                            split_high(nc.scalar.copy, u, u).then_inc(high_by["act"], 1)
                        if u % NCH == NCH - 1:
                            par = u // NCH
                            act.wait_ge(below_ready, image * T + t * 2 + par + 1)
                            nc.scalar.activation(chunk_w[:, par, :], below_max[:, par, :], ACT.Exp
                                                 ).then_inc(chunk_w_ready, 1)
                        if first and 0 < u <= NCH:
                            transposed_f(image + 2, image % 2, [u - 1])

                steps1(0, True)
                with act.Fori(1, T // 2) as t:
                    steps1(t, False)

        @block.vector
        def _(dve):
            class Chain:
                base, n = 0, 0

                def count(self, ins):
                    ins.then_inc(dve_step, 1)
                    self.n += 1

                def link(self, ins):
                    self.count(ins)
                    self.wait()

                def wait(self):
                    dve.wait_ge(dve_step, self.base + self.n)

            chain = Chain()

            nc.vector.memset(x_tr[C:C1, :], 1.0).then_inc(const_ready, 1)
            nc.vector.memset(x_abs[C:C1, :], 1.0).then_inc(const_ready, 1)
            dve.wait_ge(w_in, 16 * N_W)
            chain.link(nc.vector.tensor_reduce(w_row[:, :], w1[:, :, :], mybir.AxisListType.XY, ALU.add,
                                               apply_absolute_value=True))
            START = chain.n

            LINK_PIECES, LINK_MAX, LINK_ATT = 6, 4, 2
            LINK_BOUND, LINK_CHUNK, LINK_BELOW, LINK_W = 13, 1, 1, 5
            LINK_BLOCK = NCH * LINK_CHUNK + LINK_BELOW + LINK_W
            L0 = NCH * (LINK_MAX + LINK_ATT)
            BETWEEN = LINK_PIECES + LINK_BOUND
            PER_IMAGE = L0 + BETWEEN + T * LINK_BLOCK

            def transposed(image, layer):
                for r in range(RT):
                    dve.wait_ge(xt_ps[layer], image * RT + r + 1)
                    nc.vector.tensor_copy(half_of_blocks(r, 1), score_banks[C:P, r, :]
                                          .rearrange("c (k n) -> c k n", n=P)).then_inc(xt_dve[layer], 1)

            def block_max(chunk, blk, js, banks=2):
                for j in js:
                    dve.wait_ge(a_ready, chunk * TILES + blk * ATN + j + 1)
                    nc.vector.reduce_max(tile_max[:, blk, j:j + 1], sum_banks[:, (2 + j % banks) % 4, :], AX_X
                                         ).then_inc(a_used, 1)

            def steps0(image, q, t, chunk, first_block, behind=None, start=False):
                for u in range(U0):
                    block_max(chunk, first_block + u // 4, range(2 * (u % 4), 2 * (u % 4) + 2))
                    if behind is not None and u == LAG0:
                        attention0(image, image % 2, behind)
                    for half in range(2):
                        step = u - DVE_BEHIND - half
                        if step % U0 in LOW[0]["dve"] and not (start and step < 0):
                            low0(image, q * (T // U0) + t, step, half)

            def last_lows0(image):
                for u in range(U0, U0 + DVE_BEHIND + 1):
                    for half in range(2):
                        step = u - DVE_BEHIND - half
                        if step < U0 and step in LOW[0]["dve"]:
                            low0(image, NCH * (T // U0) - 1, step, half)

            def other_steps0(image, q):
                ahead = image * NCH + q + 1
                with dve.Fori(1, LINED_UP) as t:
                    steps0(image, q, t, ahead, EARLY + t * EARLY)
                split_max(ahead)
                steps0(image, q, LINED_UP, ahead + 1, 0)

            def low0(image, t, u, half):
                if half == 0:
                    wait_high(dve, 0, image, t, u)
                u = u % U0
                part = slice(half * BANK, (half + 1) * BANK)
                ins = nc.vector.tensor_tensor(e_low[:, u, part], probs[:, u % RING, part], e_high[:, u, part], ALU.subtract)
                if half == 1:
                    ins.then_inc(low_by["dve"], 1)

            def image_scale(image, layer, extra, gam_down):
                col = slice(layer, layer + 1)
                dve.wait_ge(v_top_ready[layer], image + 1)
                chain.link(nc.vector.tensor_scalar(v_top1[:, col], v_top[:, col], 2.0 ** -100, None, ALU.max))
                chain.link(nc.vector.tensor_scalar(v_pow2[:, col].bitcast(I32), v_top1[:, col].bitcast(I32),
                                                   EXPONENT_BITS, None, ALU.bitwise_and))
                chain.link(nc.vector.reciprocal(v_inv[:, col], v_pow2[:, col]))
                chain.link(nc.vector.tensor_scalar(gam_down, v_pow2[:, col], gammas[:, col],
                                                   2.0 ** (extra - HALF_TOP), ALU.mult, ALU.mult))
                up_ = nc.vector.tensor_scalar(v_up[:, col], v_inv[:, col], 2.0 ** (HALF_TOP - extra), None, ALU.mult)
                if layer == 0:
                    up_.then_inc(h_scale_ready, 1)
                else:
                    chain.link(up_)

            def split_max(chunk):
                dve.wait_ge(a_used, (chunk + 1) * TILES + FREE_A)
                blocks = ds(place(chunk) * BPC, BPC)
                chain.link(nc.vector.reduce_max(row_max0[:, :], tile_max[:, :, :], AX_X))
                chain.link(nc.vector.tensor_scalar(g_blocks[:, blocks, KS], row_max0[:, :], -1.0, None, ALU.mult))
                chain.link(nc.vector.scalar_tensor_tensor(max_rest[:, :], row_max0[:, :], -1.0,
                                                          g_blocks[:, blocks, KS], ALU.mult, ALU.subtract))
                chain.link(nc.vector.tensor_copy(g_blocks[:, blocks, KS + 1], max_rest[:, :]))
                nc.vector.tensor_tensor(g_blocks[:, blocks, KS + 2], max_rest[:, :], g_blocks[:, blocks, KS + 1],
                                        ALU.subtract).then_inc(max_split, 1)

            def attention0(image, par, q):
                dve.wait_ge(pv0_done, image * NCH * T + (q + 1) * T + FREE_E0)
                dve.wait_ge(x_mid_ready, image * NCH + q + FREE)
                sums = sum_banks[:, 0:2, 0:4 * VW].rearrange("p a (k c) -> p a k c", c=VW)
                chain.link(nc.vector.reciprocal(inv_sum0[:, :, :], sums[:, :, :, C]))
                chain.link(nc.vector.tensor_scalar(inv_gam0[:, :, :], inv_sum0[:, :, :], gam_down0[:, ds(par, 1)], None, ALU.mult))
                nc.vector.tensor_tensor(att0[:, :, :].rearrange("p (a k) c -> p a k c", a=2), sums[:, :, :, 0:C],
                                        inv_gam0[:, :, :].unsqueeze(3).to_broadcast([P, 2, BPC // 2, C]),
                                        ALU.mult).then_inc(att0_ready, 1)

            def rebase(value):
                chain.base, chain.n = value, 0

            def project0(image):
                transposed(image, 0)
                for r in range(1, RND, 2):
                    dve.wait_ge(pj_ps, image * RND + r + 1)
                    nc.vector.tensor_copy(proj[:, r * TR:(r + 1) * TR, 0:PW],
                                          score_banks[:, r % 4, :].rearrange("p (k n) -> p k n", k=TR)[:, :, 0:PW]
                                          ).then_inc(pj_dve, 1)

            def pieces(image):
                dve.wait_ge(pj_dve, (image + 1) * (RND // 2))
                dve.wait_ge(pj_act, (image + 1) * (RND // 2))
                src = proj[:, :, 0:GFW]
                for k in range(3):
                    nc.vector.tensor_copy(piece[k][:, :, :], src).then_inc(piece_ready, 1)
                    if k < 2:
                        dve.wait_ge(piece_ready, image * 3 + k + 1)
                        chain.link(nc.vector.tensor_tensor(src, src, piece[k][:, :, :], ALU.subtract))

            def largest_h():
                nc.vector.tensor_reduce(v_abs[:, 0:1], proj[:, :, GFW:PW], mybir.AxisListType.XY, ALU.max,
                                        apply_absolute_value=True).then_inc(v_abs_ready[0], 1)

            def transposed_g(image, par, rounds=range(NCH)):
                for r in rounds:
                    dve.wait_ge(gt_ps, image * NCH + r + 1)
                    nc.vector.tensor_copy(g_tr[0:KS, par, r * CH:(r + 1) * CH],
                                          sum_banks[0:KS, 2 * (r % 2) + 1, :].bitcast(BF16)).then_inc(gt_sb, 1)

            dve.wait_ge(const_ready, 10)
            with dve.Fori(0, 2) as image:
                rebase(image * LINK_PIECES + START)
                project0(image)
                pieces(image)
                largest_h()
                transposed_g(image, image % 2)
                image_scale(image, 0, 0, gam_down0[:, ds(image, 1)])
                assert chain.n == LINK_PIECES
            rebase(START + 2 * LINK_PIECES)
            with dve.Fori(0, BPC) as blk:
                block_max(0, blk, range(ATN), 4)
            split_max(0)
            with dve.Fori(0, EARLY) as blk:
                block_max(1, blk, range(ATN), 4)
            START += 2 * LINK_PIECES + LINK_MAX
            with dve.Fori(0, B) as image:
                start = image * PER_IMAGE + START
                par = image % 2
                steps0(image, 0, 0, image * NCH + 1, EARLY, start=True)
                with dve.Fori(0, NCH - 1) as q:
                    rebase(start + q * (LINK_MAX + LINK_ATT))
                    other_steps0(image, q)
                    steps0(image, q + 1, 0, image * NCH + q + 2, EARLY, q)
                    assert chain.n == LINK_MAX + LINK_ATT
                rebase(start + L0 - LINK_MAX - LINK_ATT)
                other_steps0(image, NCH - 1)
                last_lows0(image)
                attention0(image, par, NCH - 1)

                rebase(start + L0)
                project0(image + 2)
                transposed(image, 1)
                wait_x_tr(dve, image, 1)
                chain.link(nc.vector.tensor_reduce(x_abs[0:C, :], x_tr[0:C, :], AX_X, ALU.max, apply_absolute_value=True))
                nc.vector.tensor_tensor(bound_in[:, :], x_abs[:, :], w_row[:, :], ALU.mult).then_inc(bound_sent, 1)
                pieces(image + 2)
                dve.wait_ge(bound_ps, image + 1)
                chain.link(nc.vector.tensor_scalar(bound[:, :], sum_banks[:, 0, 0:1], 2.0 ** -100, None, ALU.max))
                chain.link(nc.vector.tensor_scalar(pow2[:, :].bitcast(I32), bound[:, :].bitcast(I32), EXPONENT_BITS,
                                                   None, ALU.bitwise_and))
                chain.link(nc.vector.reciprocal(inv_pow2[:, :], pow2[:, :]))
                chain.link(nc.vector.tensor_scalar(up[:, :], inv_pow2[:, :], 2.0 ** HALF_TOP, None, ALU.mult))
                chain.link(nc.vector.tensor_scalar(down1[:, :], pow2[:, :], 2.0 ** -HALF_TOP, None, ALU.mult))
                chain.link(nc.vector.tensor_tensor(down[:, :], down1[:, :], down1[:, :], ALU.mult))
                chain.link(nc.vector.tensor_scalar(neg_down[:, :], down[:, :], -1.0, None, ALU.mult))
                nc.vector.tensor_scalar(w1s[:, :], w1[:, :, :].rearrange("p a c -> p (a c)"), up[0:C1, 0:1], None,
                                        ALU.mult).then_inc(w1s_ready, 1)
                largest_h()
                dve.wait_ge(v1_sb, (image + 1) * NCH)
                nc.vector.tensor_reduce(v_abs[:, 1:2], v1[:, :, :], mybir.AxisListType.XY, ALU.max,
                                        apply_absolute_value=True).then_inc(v_abs_ready[1], 1)
                image_scale(image + 2, 0, 0, gam_down0[:, ds(par, 1)])
                for c in range(NQ):
                    dve.wait_ge(high_done, 2 * (image * NQ + c + 1))
                    cols = slice(c * BANK, (c + 1) * BANK)
                    nc.vector.tensor_tensor(q_split[C:P, cols], score_banks[0:C, c % 4, :], q_split[0:C, cols],
                                            ALU.subtract).then_inc(low_done, 1)
                    nc.vector.tensor_tensor(k_low[C:P, cols], score_banks[C:P, c % 4, :], k_high[C:P, cols],
                                            ALU.subtract).then_inc(low_done, 1)
                image_scale(image, 1, -EXP_UP, gam_down1[:, :])
                assert chain.n == BETWEEN

                def weigh_chunks(i, par):
                    dve.wait_ge(chunk_w_ready, image * T + i + 1)
                    dve.wait_ge(exp1_done, image * STEPS1 + (i + 1) * NCH + FREE_S1)
                    chain.link(nc.vector.tensor_tensor_reduce(
                        out=part_scr[:, :], in0=part_sum[:, par, :], in1=chunk_w[:, par, :], scale=1.0, scalar=0.0,
                        op0=ALU.mult, op1=ALU.add, accum_out=row_sum1[:, par:par + 1]))
                    chain.link(nc.vector.reciprocal(inv_sum1[:, par:par + 1], row_sum1[:, par:par + 1]))
                    chain.count(nc.vector.tensor_scalar(norm_w[:, par, :], chunk_w[:, par, :], inv_sum1[:, par:par + 1],
                                                       v_up[:, 1:2], ALU.mult, ALU.mult))

                def weigh_values(i, par):
                    dve.wait_ge(pv1_done, image * NCH * T + i * NCH + FREE_E1 - NCH)
                    chain.count(nc.vector.tensor_tensor(v_scaled[:, par, :, :],
                                                       v1[:, i, :].unsqueeze(1).to_broadcast([P, NCH, C]),
                                                       norm_w[:, par, :].unsqueeze(2).to_broadcast([P, NCH, C]), ALU.mult))

                def split_values(par):
                    chain.link(nc.vector.tensor_copy(v_high[:, par, :, :], v_scaled[:, par, :, :]))
                    nc.vector.tensor_tensor(v_low[:, par, :, :], v_scaled[:, par, :, :], v_high[:, par, :, :],
                                            ALU.subtract).then_inc(v_split_ready, 1)

                def steps1(t, first):
                    for u in range(U1):
                        k = image * NCH * T + t * U1 + u
                        par, j = u // NCH, u % NCH
                        dve.wait_ge(s_ready, k + 1)
                        chain.link(nc.vector.reduce_max(chunk_max[:, par, j:j + 1],
                                                        score_banks[:, 2 * (u % 2):2 * (u % 2) + 2, :]
                                                        .rearrange("p a n -> p (a n)"), AX_X))
                        nc.vector.tensor_scalar(exp_bias[:, u:u + 1], chunk_max[:, par, j:j + 1], neg_down[:, 0:1],
                                                LOG_UP, ALU.mult, ALU.add).then_inc(bias_ready, 1)
                        if j == NCH - 1:
                            chain.link(nc.vector.reduce_max(row_max1[:, par:par + 1], chunk_max[:, par, :], AX_X))
                            nc.vector.tensor_scalar(below_max[:, par, :], chunk_max[:, par, :],
                                                    row_max1[:, par:par + 1], down[:, 0:1], ALU.subtract, ALU.mult
                                                    ).then_inc(below_ready, 1)
                        if first and 0 < u <= NCH:
                            transposed_g(image + 2, image % 2, [u - 1])
                        if not (first and par == 0):
                            if j == 0:
                                weigh_chunks(t * 2 + par - 1, 1 - par)
                            elif j == 1:
                                weigh_values(t * 2 + par - 1, 1 - par)
                            elif j == 2:
                                split_values(1 - par)

                main = start + L0 + BETWEEN
                rebase(main)
                steps1(0, True)
                with dve.Fori(1, T // 2) as t:
                    rebase(main + t * (2 * LINK_BLOCK) - LINK_W)
                    steps1(t, False)
                    assert chain.n == 2 * LINK_BLOCK
                rebase(start + PER_IMAGE - LINK_W)
                weigh_chunks(T - 1, 1)
                chain.wait()
                weigh_values(T - 1, 1)
                chain.wait()
                split_values(1)
                dve.wait_ge(pv1_done, (image + 1) * NCH * T + FREE_E1)
                for j in range(NCH):
                    blocks = slice(j * BPC, (j + 1) * BPC)
                    nc.vector.scalar_tensor_tensor(
                        out=x_mid[:, blocks, :].rearrange("p k c -> p (k c)"), in0=sum_banks[:, j, :],
                        scalar=gam_down1[:, :], in1=x_mid[:, blocks, :].rearrange("p k c -> p (k c)"),
                        op0=ALU.mult, op1=ALU.add).then_inc(y_ready, 1)


_INS = ['x', 'L0_conv_wf', 'L0_conv_bf', 'L0_conv_wg', 'L0_conv_bg', 'L0_conv_wh', 'L0_conv_bh', 'L0_conv_gamma',
        'L1_conv_Wq', 'L1_conv_bq', 'L1_conv_Wk', 'L1_conv_bk', 'L1_conv_Wv', 'L1_conv_bv', 'L1_conv_gamma']


def kernel(**inputs):
    import numpy as _np
    import concourse.bacc as _bacc
    from concourse import mybir as _mybir
    from concourse.bass_utils import run_bass_kernel_spmd as _run

    nc = _bacc.Bacc("TRN2", target_bir_lowering=False, num_devices=1)
    arrays, args = {}, []
    for name in _INS:
        a = _np.ascontiguousarray(inputs[name])
        arrays[f"in_{name}_dram"] = a
        args.append(nc.dram_tensor(f"in_{name}_dram", a.shape, _mybir.dt.from_np(a.dtype), kind="ExternalInput").ap())
    shape = tuple(inputs['x'].shape)
    args.append(nc.dram_tensor("out_0_dram", shape, _mybir.dt.float32, kind="ExternalOutput").ap())
    attention_pair_kernel(nc, *args)
    r = _run(nc, [arrays], core_ids=[0])
    return r.results[0]["out_0_dram"]
```
